# Optimizing a Trainium2 kernel written in Bass

```python
import numpy as np
import jax
import jax.numpy as jnp

def _softmax(x, axis=-1):
    return jax.nn.softmax(x, axis=axis)

def _gelu(x):
    return jax.nn.gelu(x, approximate=True)

def _silu(x):
    return jax.nn.silu(x)

def _sigmoid(x):
    return jax.nn.sigmoid(x)

def _layernorm(x, axis=-1, eps=1e-05):
    m = jnp.mean(x, axis=axis, keepdims=True)
    v = jnp.var(x, axis=axis, keepdims=True)
    return (x - m) / jnp.sqrt(v + eps)

def _scatter_add(tgt, idx, src, axis=0):
    return tgt.at[idx].add(src)

def _segment_sum(src, seg, n):
    return jax.ops.segment_sum(src, seg, n)
kernel_name = 'mk_adj_ffn_d1_adj_r2_6c1e4a'

def setup_inputs(seed: int=0):
    np.random.seed(seed)
    _w = jnp.asarray

    def _rec_inputs():
        import jax
        import jax.numpy as jnp
        _gk = jax.random.key(seed)
        x = -0.0002928 + 1 * jax.random.normal(jax.random.fold_in(_gk, 1), (2048, 512), jnp.float32)
        _a = jax.random.bernoulli(jax.random.fold_in(_gk, 2), 0.000976562, (2048, 2048))
        _af = _a.astype(jnp.float32)
        adj = _af
        return (x, adj)
    x, adj = _rec_inputs()

    def _L0_gnn_setup():
        import jax, jax.numpy as jnp
        import numpy as np
        N = 2048
        D_IN = 512
        H = 16
        DH = D_IN // H
        ALPHA = 0.2
        MASK_VAL = -65500.0
        key = jax.random.key(seed)
        ks = jax.random.split(key, 7)
        x = jax.random.normal(ks[0], (N, D_IN), dtype=jnp.float32)
        adj = jax.random.randint(ks[1], (N, N), 0, 2).astype(jnp.float32)
        s = 1.0 / np.sqrt(D_IN)
        W_seq = jax.random.normal(ks[2], (D_IN, D_IN), dtype=jnp.float32) * s
        a1 = jax.random.normal(ks[3], (DH,), dtype=jnp.float32) / np.sqrt(DH)
        a2 = jax.random.normal(ks[4], (DH,), dtype=jnp.float32) / np.sqrt(DH)
        W_out = jax.random.normal(ks[5], (D_IN, D_IN), dtype=jnp.float32) * s
        b_out = jax.random.normal(ks[6], (D_IN,), dtype=jnp.float32) * 0.01
        return {'x': x, 'adj': adj, 'W_seq': W_seq, 'a1': a1, 'a2': a2, 'W_out': W_out, 'b_out': b_out}
    _L0_gnn_all = _L0_gnn_setup()
    _L0_gnn_in = {k: v for k, v in _L0_gnn_all.items() if k in ('W_seq', 'a1', 'a2', 'W_out', 'b_out')}
    del _L0_gnn_all

    def _L0_ffn_setup():
        import jax, jax.numpy as jnp
        import numpy as np
        import math
        B, S, D = (2, 1024, 512)
        H = 16
        HD = D // H
        FFN = 1024
        E = 8
        TOP_K = 2
        CAP_FACTOR = 1.25
        EPS = 1e-06
        BASE = 10000.0
        CAP = max(math.ceil(B * S * TOP_K * CAP_FACTOR / E), 1)

        def _rmsnorm(x, w):
            rms = jax.lax.rsqrt(jnp.mean(x * x, axis=-1, keepdims=True) + EPS)
            return w * x * rms

        def _rope(x, cos, sin):
            xr = x[..., 0::2]
            xi = x[..., 1::2]
            c = cos[None, None]
            s_ = sin[None, None]
            out_r = xr * c - xi * s_
            out_i = xr * s_ + xi * c
            return jnp.stack([out_r, out_i], axis=-1).reshape(x.shape)

        def _mha(x, w_qkv, w_o):
            b, s, d = x.shape
            qkv = x @ w_qkv
            q, k, v = jnp.split(qkv, 3, axis=-1)
            to_heads = lambda z: z.reshape(b, s, H, HD).transpose(0, 2, 1, 3)
            q, k, v = (to_heads(q), to_heads(k), to_heads(v))
            theta = BASE ** (-2.0 * (jnp.arange(HD // 2, dtype=jnp.float32) / HD))
            freqs = jnp.arange(s, dtype=jnp.float32)[:, None] * theta[None, :]
            cos, sin = (jnp.cos(freqs), jnp.sin(freqs))
            q = _rope(q, cos, sin)
            k = _rope(k, cos, sin)
            scores = jnp.einsum('bhqd,bhkd->bhqk', q, k) / jnp.sqrt(jnp.float32(HD))
            causal = jnp.tril(jnp.ones((s, s), dtype=bool))
            scores = jnp.where(causal, scores, -jnp.inf)
            attn = jax.nn.softmax(scores, axis=-1)
            y = jnp.einsum('bhqk,bhkd->bhqd', attn, v)
            y = y.transpose(0, 2, 1, 3).reshape(b, s, d)
            return y @ w_o

        def _moe(x, w_router, w1, w2):
            b, s, d = x.shape
            t = b * s
            xf = x.reshape(t, d)
            logits = xf.astype(jnp.float32) @ w_router.astype(jnp.float32)
            probs = jax.nn.softmax(logits, axis=-1)
            g, eidx = jax.lax.top_k(probs, TOP_K)
            fg = g.reshape(t * TOP_K)
            fe = eidx.reshape(t * TOP_K)
            tok_of = jnp.arange(t * TOP_K) // TOP_K
            masked = jnp.where(fe[None, :] == jnp.arange(E)[:, None], fg[None, :], -jnp.inf)
            vals, idx = jax.lax.top_k(masked, CAP)
            valid = jnp.isfinite(vals)
            gates = jnp.where(valid, vals, 0.0)
            tok = tok_of[idx]
            xe = xf[tok]
            h = jax.nn.relu(jnp.einsum('ecd,edf->ecf', xe, w1))
            ye = jnp.einsum('ecf,efd->ecd', h, w2) * gates[..., None]
            y = jnp.zeros_like(xf).at[tok.reshape(-1)].add(ye.reshape(-1, d))
            return y.reshape(b, s, d)
        key = jax.random.key(seed)
        ks = jax.random.split(key, 6)
        sd = 0.02
        return {'x': jax.random.normal(ks[0], (B, S, D), jnp.float32), 'g1': jnp.ones((D,), jnp.float32), 'w_qkv': jax.random.normal(ks[1], (D, 3 * D), jnp.float32) * sd, 'w_o': jax.random.normal(ks[2], (D, D), jnp.float32) * sd, 'g2': jnp.ones((D,), jnp.float32), 'w_router': jax.random.normal(ks[3], (D, E), jnp.float32) * sd, 'w1': jax.random.normal(ks[4], (E, D, FFN), jnp.float32) * sd, 'w2': jax.random.normal(ks[5], (E, FFN, D), jnp.float32) * sd}
    _L0_ffn_all = _L0_ffn_setup()
    _L0_ffn_in = {k: v for k, v in _L0_ffn_all.items() if k in ('g1', 'w_qkv', 'w_o', 'g2', 'w_router', 'w1', 'w2')}
    del _L0_ffn_all
    return {'x': x, 'adj': adj, 'L0_gnn_W_seq': _L0_gnn_in['W_seq'], 'L0_gnn_a1': _L0_gnn_in['a1'], 'L0_gnn_a2': _L0_gnn_in['a2'], 'L0_gnn_W_out': _L0_gnn_in['W_out'], 'L0_gnn_b_out': _L0_gnn_in['b_out'], 'L0_ffn_g1': _L0_ffn_in['g1'], 'L0_ffn_w_qkv': _L0_ffn_in['w_qkv'], 'L0_ffn_w_o': _L0_ffn_in['w_o'], 'L0_ffn_g2': _L0_ffn_in['g2'], 'L0_ffn_w_router': _L0_ffn_in['w_router'], 'L0_ffn_w1': _L0_ffn_in['w1'], 'L0_ffn_w2': _L0_ffn_in['w2']}

def reference(x, adj, L0_gnn_W_seq, L0_gnn_a1, L0_gnn_a2, L0_gnn_W_out, L0_gnn_b_out, L0_ffn_g1, L0_ffn_w_qkv, L0_ffn_w_o, L0_ffn_g2, L0_ffn_w_router, L0_ffn_w1, L0_ffn_w2):
    import jax
    import jax.numpy as jnp

    def _L0_gnn_ref(x, adj, W_seq, a1, a2, W_out, b_out):
        import jax, jax.numpy as jnp
        import numpy as np
        N = 2048
        D_IN = 512
        H = 16
        DH = D_IN // H
        ALPHA = 0.2
        MASK_VAL = -65500.0
        seq = (x @ W_seq).reshape(N, H, DH)
        score1 = jnp.einsum('nhd,d->hn', seq, a1)
        score2 = jnp.einsum('nhd,d->hn', seq, a2)
        scores = score1[:, :, None] + score2[:, None, :]
        scores = jax.nn.leaky_relu(scores, negative_slope=ALPHA)
        scores = scores + (1.0 - adj)[None, :, :] * MASK_VAL
        attn = jax.nn.softmax(scores, axis=-1)
        hidden = jnp.einsum('hij,jhd->ihd', attn, seq).reshape(N, D_IN)
        hidden = hidden @ W_out + b_out
        return jax.nn.elu(hidden)

    def _L0_ffn_ref(x, g1, w_qkv, w_o, g2, w_router, w1, w2):
        import jax, jax.numpy as jnp
        import numpy as np
        import math
        B, S, D = (2, 1024, 512)
        H = 16
        HD = D // H
        FFN = 1024
        E = 8
        TOP_K = 2
        CAP_FACTOR = 1.25
        EPS = 1e-06
        BASE = 10000.0
        CAP = max(math.ceil(B * S * TOP_K * CAP_FACTOR / E), 1)

        def _rmsnorm(x, w):
            rms = jax.lax.rsqrt(jnp.mean(x * x, axis=-1, keepdims=True) + EPS)
            return w * x * rms

        def _rope(x, cos, sin):
            xr = x[..., 0::2]
            xi = x[..., 1::2]
            c = cos[None, None]
            s_ = sin[None, None]
            out_r = xr * c - xi * s_
            out_i = xr * s_ + xi * c
            return jnp.stack([out_r, out_i], axis=-1).reshape(x.shape)

        def _mha(x, w_qkv, w_o):
            b, s, d = x.shape
            qkv = x @ w_qkv
            q, k, v = jnp.split(qkv, 3, axis=-1)
            to_heads = lambda z: z.reshape(b, s, H, HD).transpose(0, 2, 1, 3)
            q, k, v = (to_heads(q), to_heads(k), to_heads(v))
            theta = BASE ** (-2.0 * (jnp.arange(HD // 2, dtype=jnp.float32) / HD))
            freqs = jnp.arange(s, dtype=jnp.float32)[:, None] * theta[None, :]
            cos, sin = (jnp.cos(freqs), jnp.sin(freqs))
            q = _rope(q, cos, sin)
            k = _rope(k, cos, sin)
            scores = jnp.einsum('bhqd,bhkd->bhqk', q, k) / jnp.sqrt(jnp.float32(HD))
            causal = jnp.tril(jnp.ones((s, s), dtype=bool))
            scores = jnp.where(causal, scores, -jnp.inf)
            attn = jax.nn.softmax(scores, axis=-1)
            y = jnp.einsum('bhqk,bhkd->bhqd', attn, v)
            y = y.transpose(0, 2, 1, 3).reshape(b, s, d)
            return y @ w_o

        def _moe(x, w_router, w1, w2):
            b, s, d = x.shape
            t = b * s
            xf = x.reshape(t, d)
            logits = xf.astype(jnp.float32) @ w_router.astype(jnp.float32)
            probs = jax.nn.softmax(logits, axis=-1)
            g, eidx = jax.lax.top_k(probs, TOP_K)
            fg = g.reshape(t * TOP_K)
            fe = eidx.reshape(t * TOP_K)
            tok_of = jnp.arange(t * TOP_K) // TOP_K
            masked = jnp.where(fe[None, :] == jnp.arange(E)[:, None], fg[None, :], -jnp.inf)
            vals, idx = jax.lax.top_k(masked, CAP)
            valid = jnp.isfinite(vals)
            gates = jnp.where(valid, vals, 0.0)
            tok = tok_of[idx]
            xe = xf[tok]
            h = jax.nn.relu(jnp.einsum('ecd,edf->ecf', xe, w1))
            ye = jnp.einsum('ecf,efd->ecd', h, w2) * gates[..., None]
            y = jnp.zeros_like(xf).at[tok.reshape(-1)].add(ye.reshape(-1, d))
            return y.reshape(b, s, d)
        x = x + _mha(_rmsnorm(x, g1), w_qkv, w_o)
        x = x + _moe(_rmsnorm(x, g2), w_router, w1, w2)
        return x
    x = x + _L0_gnn_ref(_layernorm(x, axis=-1), adj, L0_gnn_W_seq, L0_gnn_a1, L0_gnn_a2, L0_gnn_W_out, L0_gnn_b_out)
    x = x + _L0_ffn_ref(_layernorm(x, axis=-1)[None], L0_ffn_g1, L0_ffn_w_qkv, L0_ffn_w_o, L0_ffn_g2, L0_ffn_w_router, L0_ffn_w1, L0_ffn_w2)[0]
    return x

_drawn_inputs = setup_inputs


def setup_inputs(seed=0):
    import zlib

    import numpy as np

    out = dict(_drawn_inputs(seed))
    spreads = {'L0_ffn_g1': (1.0, 0.6), 'L0_ffn_g2': (1.0, 0.6)}
    factors = {'L0_gnn_b_out': 7.286,
     'L0_ffn_w_qkv': 7.635,
     'L0_ffn_w_o': 7.404,
     'L0_ffn_w_router': 8.0,
     'L0_ffn_w1': 8.0,
     'L0_ffn_w2': 8.0}
    for name, (base, spread) in spreads.items():
        noise = np.random.default_rng([zlib.crc32(name.encode()), seed]).standard_normal(out[name].shape)
        drawn = base * np.exp(spread * noise) if base else spread * noise
        out[name] = jnp.asarray(drawn.astype(out[name].dtype))
    for name, factor in factors.items():
        out[name] = (out[name] * factor).astype(out[name].dtype)
    return out
```

```python
from contextlib import ExitStack

import concourse.bass as bass
import numpy as np
from concourse import mybir

F32 = mybir.dt.float32
F32R = mybir.dt.float32r
BF16 = mybir.dt.bfloat16
I32 = mybir.dt.int32
U32 = mybir.dt.uint32
ALU = mybir.AluOpType
ACT = mybir.ActivationFunctionType
AX = mybir.AxisListType.X
ds = bass.ds

P = 128
N, D = 2048, 512
T = N // P
KD = D // P
H, DH = 16, 32
LN_EPS, RMS_EPS = 1e-5, 1e-6
ALPHA = 0.2
BANK = 512


class Stage:

    def __init__(self, nc, name):
        self.nc, self.name, self.ctx = nc, name, ExitStack()

    def __enter__(self):
        self.ctx.__enter__()
        return self

    def __exit__(self, *a):
        return self.ctx.__exit__(*a)

    def sb(self, name, shape, dt=F32):
        return self.ctx.enter_context(self.nc.sbuf_tensor(f"{self.name}_{name}", shape, dt))

    def ps(self, name, shape, dt=F32):
        return self.ctx.enter_context(self.nc.psum_tensor(f"{self.name}_{name}", shape, dt))


class Link:

    def __init__(self, eng, sem):
        self.eng, self.sem, self.n = eng, sem, 0

    def __call__(self, ins):
        self.n += 1
        ins.then_inc(self.sem, 1)
        self.eng.wait_ge(self.sem, self.n)

    def restart(self):
        self.eng.sem_clear(self.sem)
        self.n = 0


def stage_sequence(nc, sem, keep, x, adj, w_seq, a1, a2):
    seq, adjT, s1, s2 = keep["seq"], keep["adjT"], keep["s1"], keep["s2"]
    with Stage(nc, "a") as st:
        X = keep["part"][:, :, :, :].rearrange("p t h c -> p (t h c)")[:, 0:T * D]
        X = X.rearrange("p (t d) -> p t d", t=T)
        xT = st.sb("xT", [P, KD, N])
        W = st.sb("w", [P, KD, D])
        arow = [st.sb("row1", [P, DH]), st.sb("row2", [P, DH])]
        stats = st.sb("stats", [P, T, 6])
        mv = st.sb("mv", [P, T, 2])
        ve, sd, rstd = (st.sb(n, [P, T]) for n in ("ve", "sd", "rstd"))
        prod = [st.sb(f"prod{i}", [P, H, DH]) for i in range(2)]
        adj_in = [st.sb(f"adj{i}", [P, N]) for i in range(2)]
        adj_b = [st.sb(f"adjb{i}", [P, N], BF16) for i in range(2)]
        degree = [st.sb(f"degree{i}", [P, 1]) for i in range(2)]
        alone = [st.sb(f"alone{i}", [P, 1]) for i in range(2)]
        ps_t = [st.ps(f"t{i}", [P, BANK]) for i in range(2)]
        ps_s = [st.ps(f"s{i}", [P, BANK]) for i in range(2)]
        ps_a = [st.ps(f"adj_t{i}", [P, N], BF16) for i in range(2)]
        x_in = [sem(f"a_x_in{i}") for i in range(4)]
        w_in, a_in = sem("a_w_in"), sem("a_a_in")
        link, sd_ready, ve_ready = sem("a_link"), sem("a_sd_ready"), sem("a_ve_ready")
        stats_done, xn_ready, xT_full, xT_ready = (sem("a_" + n) for n in ("stats", "xn", "xTf", "xTr"))
        seq_full, seq_ready, prod_done = sem("a_seqf"), sem("a_seqr"), sem("a_prod")
        adj_loaded = [sem(f"a_adj_loaded{i}") for i in range(2)]
        adj_cast = sem("a_adj_cast")
        adj_ready = [sem(f"a_adj_ready{i}") for i in range(2)]
        turned = [sem(f"a_turned{i}") for i in range(2)]
        stored = [sem(f"a_stored{i}") for i in range(2)]
        ident, ident_b = keep["ident"], keep["ident_b"]
        consts = keep["consts_ready"]
        with nc.Block() as block:

            @block.sync
            def _(sp):
                xv = x.rearrange("(t p) d -> p t d", p=P)
                for c in range(4):
                    sp.dma_start(X[:, 4 * c:4 * c + 4, :], xv[:, 4 * c:4 * c + 4, :]).then_inc(x_in[c], 16)
                sp.dma_start(W[:, :, :], w_seq.rearrange("(k p) n -> p k n", p=P)).then_inc(w_in, 16)
                for a, dst in ((a1, arow[0]), (a2, arow[1])):
                    sp.dma_start(dst[:, :], a.partition_broadcast(P)).then_inc(a_in, 16)
                for t in range(T):
                    if t >= 2:
                        sp.wait_ge(adj_cast, t - 1)
                    sp.dma_start(adj_in[t % 2][:, :], adj[t * P:(t + 1) * P, :]).then_inc(adj_loaded[t % 2], 16)

            @block.gpsimd
            def _(pool):
                pool.memset(ident[:, :], 0.0).then_inc(consts, 1)
                pool.memset(ident_b[:, :], 0.0).then_inc(consts, 1)
                pool.wait_ge(consts, 2)
                for m in (ident, ident_b):
                    pool.affine_select(out=m[:, :], in_=m[:, :], compare_op=ALU.not_equal, fill=1.0,
                                       base=0, pattern=[[-1, P]], channel_multiplier=1).then_inc(consts, 1)

            @block.scalar
            def _(act):
                def cast(t):
                    r = t % 2
                    act.wait_ge(adj_loaded[r], t // 2 * 16 + 16)
                    if t >= 2:
                        act.wait_ge(turned[r], t // 2)
                    act.activation(adj_b[r][:, :], adj_in[r][:, :], ACT.Copy, accum_out=degree[r][:, :]).then_inc(adj_cast, 1)

                def store(t):
                    act.wait_ge(turned[t % 2], t // 2 + 1)
                    act.activation(adjT[:, :, t * P:(t + 1) * P],
                                   ps_a[t % 2][:, :].rearrange("p (j q) -> p j q", q=P),
                                   ACT.Copy).then_inc(stored[t % 2], 1)

                act.wait_ge(ve_ready, 1)
                act.activation(sd[:, :], ve[:, :], ACT.Sqrt).then_inc(sd_ready, 1)
                for t in range(T):
                    act.wait_ge(xT_full, t + 1)
                    act.activation(xT[:, :, t * P:(t + 1) * P],
                                   ps_t[t % 2][:, :].rearrange("p (k q) -> p k q", q=P),
                                   ACT.Copy).then_inc(xT_ready, 1)
                    cast(t)
                    if t >= 1:
                        store(t - 1)
                store(T - 1)

            @block.vector
            def _(dve):
                lk = Link(dve, link)
                for t in range(T):
                    if t % 4 == 0:
                        dve.wait_ge(x_in[t // 4], 16)
                    dve.bn_stats(stats[:, t, :], X[:, t, :]).then_inc(stats_done, 1)
                dve.wait_ge(stats_done, T)
                for t in range(T):
                    last = dve.bn_aggr(mv[:, t, :], stats[:, t, :])
                lk(last)
                dve.tensor_scalar(ve[:, :], mv[:, :, 1], LN_EPS, None, ALU.add).then_inc(ve_ready, 1)
                dve.wait_ge(sd_ready, 1)
                root_of_inverse(dve, lk, rstd, sd, ve)
                for t in range(T):
                    dve.tensor_scalar(X[:, t, :], X[:, t, :], mv[:, t, 0:1], rstd[:, t:t + 1],
                                      ALU.subtract, ALU.mult).then_inc(xn_ready, 1)
                dve.wait_ge(a_in, 32)
                for t in range(T):
                    dve.wait_ge(adj_cast, t + 1)
                    lk(dve.tensor_scalar(alone[t % 2][:, :], degree[t % 2][:, :], 0.0, None, ALU.is_le))
                    dve.tensor_scalar(adj_b[t % 2][:, :], adj_b[t % 2][:, :], alone[t % 2][:, :], None,
                                      ALU.max).then_inc(adj_ready[t % 2], 1)
                    dve.wait_ge(seq_full, t + 1)
                    dve.tensor_copy(seq[:, t, :], ps_s[t % 2][:, :]).then_inc(seq_ready, 1)
                    dve.wait_ge(seq_ready, t + 1)
                    sv = seq[:, t, :].rearrange("p (h d) -> p h d", h=H)
                    for n in range(2):
                        dve.tensor_tensor(prod[n][:, :, :], sv, arow[n][:, None, :].to_broadcast([P, H, DH]),
                                          ALU.mult).then_inc(prod_done, 1)
                    for n, s in enumerate((s1, s2)):
                        dve.wait_ge(prod_done, 4 * t + n + 1)
                        dve.tensor_reduce(s[:, t, :], prod[n][:, :, :], AX, ALU.add).then_inc(prod_done, 1)
                    dve.wait_ge(prod_done, 4 * t + 4)

            @block.tensor
            def _(pe):
                def product(t):
                    pe.wait_ge(xT_ready, t + 1)
                    if t == 0:
                        pe.wait_ge(w_in, 16)
                    if t >= 2:
                        pe.wait_ge(seq_ready, t - 1)
                    for k in range(KD):
                        mm = pe.matmul(ps_s[t % 2][:, :], xT[:, k, t * P:(t + 1) * P], W[:, k, :],
                                       start=(k == 0), stop=(k == KD - 1))
                    mm.then_inc(seq_full, 1)

                def turn(t):
                    r = t % 2
                    pe.wait_ge(adj_ready[r], t // 2 + 1)
                    if t >= 2:
                        pe.wait_ge(stored[r], t // 2)
                    for j in range(T):
                        mm = pe.transpose(ps_a[r][:, j * P:(j + 1) * P], adj_b[r][:, j * P:(j + 1) * P], ident_b[:, :])
                    mm.then_inc(turned[r], 1)

                pe.wait_ge(consts, 4)
                for t in range(T):
                    pe.wait_ge(xn_ready, t + 1)
                    if t >= 2:
                        pe.wait_ge(xT_ready, t - 1)
                    for k in range(KD):
                        mm = pe.transpose(ps_t[t % 2][:, k * P:(k + 1) * P], X[:, t, k * P:(k + 1) * P], ident[:, :])
                    mm.then_inc(xT_full, 1)
                    if t >= 1:
                        product(t - 1)
                        turn(t - 1)
                product(T - 1)
                turn(T - 1)


def root_of_inverse(dve, lk, out, root, value):
    lk(dve.reciprocal(out[:, :], root[:, :]))
    lk(dve.tensor_tensor(out[:, :], out[:, :], value[:, :], ALU.mult))
    lk(dve.tensor_tensor(out[:, :], out[:, :], root[:, :], ALU.add))
    lk(dve.tensor_scalar(out[:, :], out[:, :], 0.5, None, ALU.mult))
    lk(dve.reciprocal(out[:, :], out[:, :]))


def stage_factors(nc, sem, keep, s1_dram):
    s1, s2, ident = keep["s1"], keep["s2"], keep["ident"]
    fA, fB, fC, fD, ns2 = (keep[n] for n in ("A", "B", "C", "D", "ns2"))
    with Stage(nc, "f") as st:
        pm = st.sb("pm", [P, H])
        gm = st.sb("gm", [H, 1])
        dg = st.sb("dg", [H, H])
        ones = st.sb("ones", [H, P])
        M = st.sb("M", [P, H])
        sv, u, m, am, cm = (st.sb(n, [P, T, H]) for n in ("sv", "u", "m", "am", "cm"))
        s1h = st.sb("s1h", [P, H, T])
        s1r = st.sb("s1r", [P, 2, P])
        p0, p1, p2 = (st.ps(f"p{i}", [P, BANK]) for i in range(3))
        link, pm_ready, pmT, dg_ready, M_full = (sem("f_" + n) for n in ("link", "pm", "pmT", "dg", "M"))
        sv_ready, ac_ready, s1h_ready, s1T, s1r_ready, s1_out = (
            sem("f_" + n) for n in ("sv", "ac", "s1h", "s1T", "s1r", "s1out"))
        with nc.Block() as block:

            @block.vector
            def _(dve):
                lk = Link(dve, link)
                dve.tensor_copy(s1h[:, :, :], s1[:, :, :].rearrange("p t h -> p h t")).then_inc(s1h_ready, 1)
                lk(dve.memset(ones[:, :], 1.0))
                dve.tensor_reduce(pm[:, :], s2[:, :, :].rearrange("p t h -> p h t"), AX, ALU.max).then_inc(pm_ready, 1)
                dve.tensor_scalar(ns2[:, :, :], s2[:, :, :], -1.0, None, ALU.mult)
                dve.wait_ge(pmT, 1)
                lk(dve.tensor_reduce(gm[:, :], p0[0:H, 0:P], AX, ALU.max))
                dve.tensor_scalar(dg[:, :], ident[0:H, 0:H], gm[:, :], None, ALU.mult).then_inc(dg_ready, 1)
                dve.wait_ge(s1T, 1)
                dve.tensor_copy(s1r[:, :, :], p2[:, 0:2 * P].rearrange("p (c q) -> p c q", q=P)).then_inc(s1r_ready, 1)
                dve.wait_ge(M_full, 1)
                lk(dve.tensor_copy(M[:, :], p1[:, 0:H]))
                Mb = M[:, None, :].to_broadcast([P, T, H])
                dve.tensor_tensor(sv[:, :, :], s2[:, :, :], Mb, ALU.subtract).then_inc(sv_ready, 1)
                lk(dve.tensor_tensor(u[:, :, :], s1[:, :, :], Mb, ALU.add))
                lk(dve.scalar_tensor_tensor(m[:, :, :], u[:, :, :], ALPHA, u[:, :, :], ALU.mult, ALU.max))
                dve.tensor_tensor(am[:, :, :], u[:, :, :], m[:, :, :], ALU.subtract)
                dve.scalar_tensor_tensor(cm[:, :, :], u[:, :, :], ALPHA, m[:, :, :], ALU.mult,
                                         ALU.subtract).then_inc(ac_ready, 1)

            @block.scalar
            def _(act):
                act.wait_ge(sv_ready, 1)
                act.activation(fB[:, :, :], sv[:, :, :], ACT.Exp)
                act.activation(fD[:, :, :], sv[:, :, :], ACT.Exp, scale=ALPHA)
                act.wait_ge(ac_ready, 1)
                act.activation(fA[:, :, :], am[:, :, :], ACT.Exp)
                act.activation(fC[:, :, :], cm[:, :, :], ACT.Exp)

            @block.tensor
            def _(pe):
                pe.wait_ge(pm_ready, 1)
                pe.transpose(p0[0:H, 0:P], pm[:, :], ident[:, :]).then_inc(pmT, 1)
                pe.wait_ge(s1h_ready, 1)
                sh = s1h[:, :, :].rearrange("p h t -> p (h t)")
                for c in range(2):
                    mm = pe.transpose(p2[:, c * P:(c + 1) * P], sh[:, c * P:(c + 1) * P], ident[:, :])
                mm.then_inc(s1T, 1)
                pe.wait_ge(link, 1)
                pe.wait_ge(dg_ready, 1)
                pe.matmul(p1[:, 0:H], ones[:, :], dg[:, :], start=True, stop=True).then_inc(M_full, 1)

            @block.sync
            def _(sp):
                sp.wait_ge(s1r_ready, 1)
                sp.dma_start(s1_dram.rearrange("(c r) q -> r c q", c=2), s1r[:, :, :]).then_inc(s1_out, 16)
                sp.wait_ge(s1_out, 16)


W1 = DH + 1
G4 = 4


def stage_adjacency_product(nc, sem, keep):
    seq, adjT, part, fD = keep["seq"], keep["adjT"], keep["part"], keep["D"]
    C = G4 * W1
    with Stage(nc, "g") as st:
        R = st.sb("R", [P, T, G4, W1])
        S = [st.sb(f"S{i}", [P, T, 3, C], BF16) for i in range(2)]
        acc = [st.ps(f"acc{i}", [P, BANK]) for i in range(4)]
        link = sem("g_link")
        split = [sem(f"g_split{i}") for i in range(2)]
        used = [sem(f"g_used{i}") for i in range(2)]
        full, summed = sem("g_full"), sem("g_summed")
        Rc = R[:, :, :, :].rearrange("p t g c -> p t (g c)")
        with nc.Block() as block:

            @block.tensor
            def _(pe):
                for g in range(H // G4):
                    r = g % 2
                    pe.wait_ge(split[r], g // 2 + 1)
                    for t in range(T):
                        n = g * T + t
                        if n >= 4:
                            pe.wait_ge(summed, n - 3)
                        for j in range(T):
                            mm = pe.matmul(acc[n % 4][:, 0:3 * C], adjT[:, j, t * P:(t + 1) * P],
                                           S[r][:, j, :, :].rearrange("p s c -> p (s c)"),
                                           start=(j == 0), stop=(j == T - 1))
                        mm.then_inc(full, 1)
                    pe.wait_ge(full, (g + 1) * T)
                    pe.sem_inc(used[r], 1)

            @block.vector
            def _(dve):
                lk = Link(dve, link)

                def split_group(g):
                    r = g % 2
                    for q in range(G4):
                        h = G4 * g + q
                        dcol = fD[:, :, h:h + 1]
                        dve.tensor_tensor(R[:, :, q, 0:DH], seq[:, :, h * DH:(h + 1) * DH],
                                          dcol.to_broadcast([P, T, DH]), ALU.mult)
                        last = dve.tensor_copy(R[:, :, q, DH:W1], dcol)
                    lk(last)
                    if g >= 2:
                        dve.wait_ge(used[r], g // 2)
                    for n in range(3):
                        lk(dve.tensor_copy(S[r][:, :, n, :], Rc))
                        if n < 2:
                            lk(dve.tensor_tensor(Rc, Rc, S[r][:, :, n, :], ALU.subtract))
                    dve.sem_inc(split[r], 1)

                split_group(0)
                for g in range(H // G4):
                    for t in range(T):
                        if t == 2 and g + 1 < H // G4:
                            split_group(g + 1)
                        n = g * T + t
                        dve.wait_ge(full, n + 1)
                        dve.tensor_reduce(part[:, t, G4 * g:G4 * g + G4, :].rearrange("p g c -> p (g c)"),
                                          acc[n % 4][:, 0:3 * C].rearrange("p (s c) -> p c s", s=3),
                                          AX, ALU.add).then_inc(summed, 1)


HALF = N // 2
SLOTS = 8
SIGNS = 4
BY_ACT = tuple(j for j in range(T) if j % 5 != 2)


def stage_masks(nc, sem, keep, s1_dram):
    seq, adjT, part = keep["seq"], keep["adjT"], keep["part"]
    fA, fB, fC, fD, s2, ns2 = (keep[n] for n in ("A", "B", "C", "D", "s2", "ns2"))
    C = 2 * W1
    with Stage(nc, "m") as st:
        s1b = [st.sb(f"s1b{i}", [P, N]) for i in range(2)]
        R = [st.sb(f"R{i}", [P, T, C]) for i in range(2)]
        cols = [st.sb(f"cols{i}", [P, 4, T, 1]) for i in range(2)]
        S = [st.sb(f"S{i}", [P, T, 3, C], BF16) for i in range(2)]
        mask = [st.sb(f"mask{i}", [P, HALF], BF16) for i in range(SLOTS)]
        sign = [st.sb(f"sign{i}", [P, HALF], BF16) for i in range(SIGNS)]
        G = [st.sb(f"G{i}", [P, T // 2, C]) for i in range(2)]
        U = st.sb("U", [P, T // 2, W1])
        V = st.sb("V", [P, T // 2, W1])
        rc = st.sb("rc", [P, T // 2, 1])
        acc = [st.ps(f"acc{i}", [P, BANK]) for i in range(8)]
        s1_in = [sem(f"m_s1_in{i}") for i in range(2)]
        s1_free = [sem(f"m_s1_free{i}") for i in range(2)]
        s1_free_act = [sem(f"m_s1_fra{i}") for i in range(2)]
        split = [sem(f"m_split{i}") for i in range(2)]
        rest = [sem(f"m_rest{i}") for i in range(2)]
        weighed = [sem(f"m_weighed{i}") for i in range(2)]
        masks_made = [sem(f"m_masks_made{i}") for i in range(2)]
        link, dlink = sem("m_link"), sem("m_dlink")
        mask_ready, mask_free = sem("m_mask_ready"), sem("m_mask_free")
        sign_ready, sign_free = sem("m_sign_ready"), sem("m_sign_free")
        full = [sem(f"m_full{i}") for i in range(2)]
        summed = [sem(f"m_summed{i}") for i in range(2)]
        merged = [sem(f"m_merged{i}") for i in range(2)]
        UNITS = 4
        NA = len(BY_ACT)
        with nc.Block() as block:

            @block.sync
            def _(sp):
                rows = s1_dram.rearrange("(h t) q -> h (t q)", h=H)
                with sp.Fori(0, H // 2) as i:
                    for r in range(2):
                        sp.wait_ge(s1_free[r], i + 1)
                        sp.wait_ge(s1_free_act[r], i + 1)
                        src = rows[ds(i * 2 + r, 1), :]
                        sp.dma_start(s1b[r][:, :], src.to_broadcast([P, N])).then_inc(s1_in[r], 16)

            @block.gpsimd
            def _(pool):
                lk = Link(pool, link)

                def weigh_head(h, r):
                    bcol, dcol = fB[:, :, ds(h, 1)], fD[:, :, ds(h, 1)]
                    sh = seq[:, :, ds(h * DH, DH)]
                    pool.tensor_tensor(R[r][:, :, 0:DH], sh, bcol.to_broadcast([P, T, DH]), ALU.mult)
                    pool.tensor_copy(R[r][:, :, DH:W1], bcol)
                    pool.tensor_tensor(R[r][:, :, W1:W1 + DH], sh, dcol.to_broadcast([P, T, DH]), ALU.mult)
                    pool.tensor_copy(R[r][:, :, W1 + DH:C], dcol)
                    for n, f in enumerate((fA, fC, s2, ns2)):
                        last = pool.tensor_copy(cols[r][:, n, :, :], f[:, :, ds(h, 1)])
                    lk(last)
                    pool.sem_inc(weighed[r], 1)

                def merge_unit(h, half, u, turn):
                    b, r = u % 2, u // 2
                    rows = slice(half * T // 2, (half + 1) * T // 2)
                    pool.wait_ge(summed[b], turn + 1)
                    g = G[b]
                    pt = part[:, rows, ds(h, 1), :].rearrange("p t h c -> p t (h c)")
                    a_ = cols[r][:, 0, rows, :].to_broadcast([P, T // 2, W1])
                    c_ = cols[r][:, 1, rows, :].to_broadcast([P, T // 2, W1])
                    pool.tensor_tensor(V[:, :, :], g[:, :, 0:W1], a_, ALU.mult)
                    lk(pool.tensor_tensor(U[:, :, :], pt, g[:, :, W1:C], ALU.subtract))
                    lk(pool.tensor_tensor(U[:, :, :], U[:, :, :], c_, ALU.mult))
                    lk(pool.tensor_tensor(pt, U[:, :, :], V[:, :, :], ALU.add))
                    pool.sem_inc(merged[b], 1)

                for b in range(2):
                    pool.sem_inc(merged[b], 1)
                def take_off(r, turn):
                    for n in range(2):
                        pool.wait_ge(split[r], (turn - 1) * 3 + n + 1)
                        pool.tensor_tensor(R[r][:, :, :], R[r][:, :, :], S[r][:, :, n, :], ALU.subtract).then_inc(rest[r], 1)

                weigh_head(0, 0)
                take_off(0, 1)
                weigh_head(1, 1)
                with pool.Fori(0, H // 2 - 1) as i:
                    lk.restart()
                    for r in range(2):
                        merge_unit(i * 2 + r, 0, 2 * r, i * 2 + r + 1)
                        take_off(1 - r, i + 1 + r)
                        merge_unit(i * 2 + r, 1, 2 * r + 1, i * 2 + r + 1)
                        pool.wait_ge(masks_made[r], i + 1)
                        weigh_head(i * 2 + r + 2, r)
                lk.restart()
                for r in range(2):
                    merge_unit(H - 2 + r, 0, 2 * r, H - 2 + r + 1)
                    if r == 0:
                        take_off(1, H // 2)
                    merge_unit(H - 2 + r, 1, 2 * r + 1, H - 2 + r + 1)

            @block.scalar
            def _(act):
                with act.Fori(0, H // 2) as i:
                    for u in range(UNITS):
                        r, half = u // 2, u % 2
                        if half == 0:
                            act.wait_ge(weighed[r], i + 1)
                            act.wait_ge(s1_in[r], i * 16 + 16)
                        for n, j in enumerate(BY_ACT):
                            k = u * NA + n
                            act.wait_ge(sign_free, i * (UNITS * NA) + k + 1)
                            act.activation(sign[k % SIGNS][:, :], s1b[r][:, half * HALF:(half + 1) * HALF],
                                           ACT.Sign, bias=cols[r][:, 2, j, :]).then_inc(sign_ready, 1)
                        if half == 1:
                            act.wait_ge(sign_ready, i * (UNITS * NA) + (u + 1) * NA)
                            act.sem_inc(s1_free_act[r], 1)

            @block.vector
            def _(dve):
                lk = Link(dve, dlink)
                for j in range(T):
                    last = dve.tensor_scalar(adjT[:, j, :], adjT[:, j, :], -1.0, 1.0, ALU.mult, ALU.add)
                lk(last)
                dve.sem_inc(sign_free, SIGNS)
                for r in range(2):
                    dve.sem_inc(s1_free[r], 1)
                    dve.sem_inc(s1_free_act[r], 1)

                def split_head(r, turn, n):
                    if n == 0:
                        dve.wait_ge(weighed[r], turn)
                    else:
                        dve.wait_ge(rest[r], (turn - 1) * 2 + n)
                    dve.tensor_copy(S[r][:, :, n, :], R[r][:, :, :]).then_inc(split[r], 1)

                def splits(r, turn):
                    return {j: (lambda n=n: split_head(r, turn, n)) for n, j in enumerate((3, 9, 14))}

                def add_parts(turn, u):
                    b = u % 2
                    dve.wait_ge(full[b], turn)
                    dve.wait_ge(merged[b], turn)
                    for q in range(4):
                        last = dve.tensor_reduce(
                            G[b][:, 2 * q:2 * q + 2, :],
                            acc[4 * b + q][:, 0:6 * C].rearrange("p (t s c) -> p t c s", t=2, s=3),
                            AX, ALU.add)
                    lk(last)
                    dve.sem_inc(summed[b], 1)

                def masks(i, u, between=None):
                    r, half = u // 2, u % 2
                    cut = slice(half * HALF, (half + 1) * HALF)
                    if half == 0:
                        dve.wait_ge(weighed[r], i + 1)
                        dve.wait_ge(s1_in[r], i * 16 + 16)
                    for j in range(T):
                        if between and j in between:
                            between[j]()
                        n = u * T + j
                        dve.wait_ge(mask_free, i * (UNITS * T) + n + 1)
                        if j in BY_ACT:
                            k = u * NA + BY_ACT.index(j)
                            dve.wait_ge(sign_ready, i * (UNITS * NA) + k + 1)
                            dve.tensor_tensor(mask[n % SLOTS][:, :], sign[k % SIGNS][:, :], adjT[:, j, cut],
                                              ALU.is_gt).then_inc(mask_ready, 1)
                        else:
                            dve.scalar_tensor_tensor(mask[n % SLOTS][:, :], s1b[r][:, cut],
                                                     cols[r][:, 3, j, :], adjT[:, j, cut],
                                                     ALU.is_gt, ALU.is_gt).then_inc(mask_ready, 1)
                        if j - 1 in BY_ACT:
                            dve.wait_ge(mask_ready, i * (UNITS * T) + n)
                            dve.sem_inc(sign_free, 1)
                    dve.wait_ge(mask_ready, i * (UNITS * T) + (u + 1) * T)
                    if T - 1 in BY_ACT:
                        dve.sem_inc(sign_free, 1)
                    if half == 1:
                        dve.sem_inc(s1_free[r], 1)
                        dve.sem_inc(masks_made[r], 1)

                for b in range(2):
                    dve.sem_inc(summed[b], 1)
                for n in range(3):
                    split_head(0, 1, n)
                masks(0, 0)
                last_turn = H // 2 - 1
                with dve.Fori(0, last_turn) as i:
                    lk.restart()
                    masks(i, 1, {2: lambda: add_parts(i + i + 1, 0), **splits(1, i + 1)})
                    masks(i, 2, {2: lambda: add_parts(i + i + 1, 1)})
                    masks(i, 3, {2: lambda: add_parts(i + i + 2, 2), **splits(0, i + 2)})
                    masks(i + 1, 0, {2: lambda: add_parts(i + i + 2, 3)})
                i = last_turn
                lk.restart()
                masks(i, 1, {2: lambda: add_parts(i + i + 1, 0), **splits(1, i + 1)})
                masks(i, 2, {2: lambda: add_parts(i + i + 1, 1)})
                masks(i, 3, {2: lambda: add_parts(i + i + 2, 2)})
                add_parts(i + i + 2, 3)

            @block.tensor
            def _(pe):
                pe.sem_inc(mask_free, SLOTS)
                with pe.Fori(0, H // 2) as i:
                    for u in range(UNITS):
                        r, b = u // 2, u % 2
                        if b == 0:
                            pe.wait_ge(split[r], i * 3 + 3)
                        pe.wait_ge(summed[b], i * 2 + u // 2 + 1)
                        for j in range(T):
                            n = u * T + j
                            pe.wait_ge(mask_ready, i * (UNITS * T) + n + 1)
                            for q in range(T // 2):
                                mm = pe.matmul(acc[4 * b + q // 2][:, (q % 2) * 3 * C:(q % 2 + 1) * 3 * C],
                                               mask[n % SLOTS][:, q * P:(q + 1) * P],
                                               S[r][:, j, :, :].rearrange("p s c -> p (s c)"),
                                               start=(j == 0 and q % 2 == 0), stop=(j == T - 1 and q % 2 == 1),
                                               skip_group_check=True)
                            mm.then_inc(mask_free, 1)
                        pe.wait_ge(mask_free, i * (UNITS * T) + (u + 1) * T + SLOTS)
                        pe.sem_inc(full[b], 1)


def stage_gnn_output(nc, sem, keep, x, w_out, b_out, g1, xe_dram):
    part, X1, xgT, mv, rstd, ident = (keep[n] for n in ("part", "X1", "xgT", "mv", "rstd", "ident"))
    with Stage(nc, "o") as st:
        W = st.sb("w", [P, KD, D])
        brow, grow = st.sb("brow", [P, D]), st.sb("grow", [P, D])
        Y = st.sb("y", [P, T, D])
        rden = st.sb("rden", [P, T, H])
        hn = [st.sb(f"hn{i}", [P, D]) for i in range(2)]
        hT = [st.sb(f"hT{i}", [P, KD, P]) for i in range(2)]
        v = [st.sb(f"v{i}", [P, D]) for i in range(2)]
        low = [st.sb(f"low{i}", [P, D]) for i in range(2)]
        square = st.sb("square", [P, D])
        zeros = st.sb("zeros", [P, 4 * D])
        zeroed, cleared = sem("o_zeroed"), sem("o_cleared")
        stats = st.sb("stats", [P, T, 6])
        ve, sd, ms, rms = (st.sb(n, [P, T]) for n in ("ve", "sd", "ms", "rms"))
        ps_t = [st.ps(f"t{i}", [P, BANK]) for i in range(2)]
        ps_s = [st.ps(f"s{i}", [P, BANK]) for i in range(2)]
        x_in = [sem(f"o_x_in{i}") for i in range(4)]
        w_in, row_in = sem("o_w_in"), sem("o_row_in")
        link, hn_ready, hT_full, hT_ready, full, low_ready, exp_ready, x1_ready = (
            sem("o_" + n) for n in ("link", "hn", "hTf", "hTr", "full", "low", "exp", "x1"))
        ve_ready, sd_ready, y_ready, ms_ready, xg_ready, t_full, t_ready = (
            sem("o_" + n) for n in ("ve", "sd", "y", "ms", "xg", "tf", "tr"))
        with nc.Block() as block:

            @block.sync
            def _(sp):
                sp.dma_start(W[:, :, :], w_out.rearrange("(k p) n -> p k n", p=P)).then_inc(w_in, 16)
                sp.dma_start(brow[:, :], b_out.partition_broadcast(P)).then_inc(row_in, 16)
                sp.dma_start(grow[:, :], g1.partition_broadcast(P)).then_inc(row_in, 16)
                xv = x.rearrange("(t p) d -> p t d", p=P)
                for c in range(4):
                    sp.dma_start(X1[:, 4 * c:4 * c + 4, :], xv[:, 4 * c:4 * c + 4, :]).then_inc(x_in[c], 16)

            @block.gpsimd
            def _(pool):
                pool.memset(zeros[:, :], 0.0).then_inc(zeroed, 1)
                pool.wait_ge(zeroed, 1)
                for c in range(EXPERTS * CAP // (4 * P)):
                    pool.dma_start(xe_dram[c * 4 * P:(c + 1) * 4 * P, :].rearrange("(p r) d -> p (r d)", r=4),
                                   zeros[:, :]).then_inc(cleared, 16)
                pool.wait_ge(cleared, 16 * (EXPERTS * CAP // (4 * P)))

            @block.scalar
            def _(act):
                for t in range(T):
                    act.wait_ge(hT_full, t + 1)
                    act.activation(hT[t % 2][:, :, :], ps_t[t % 2][:, :].rearrange("p (k q) -> p k q", q=P),
                                   ACT.Copy).then_inc(hT_ready, 1)
                    if t >= 1:
                        act.wait_ge(low_ready, t)
                        act.activation(low[(t - 1) % 2][:, :], low[(t - 1) % 2][:, :], ACT.Exp).then_inc(exp_ready, 1)
                act.wait_ge(low_ready, T)
                act.activation(low[(T - 1) % 2][:, :], low[(T - 1) % 2][:, :], ACT.Exp).then_inc(exp_ready, 1)
                act.wait_ge(ve_ready, 1)
                act.activation(sd[:, :], ve[:, :], ACT.Sqrt).then_inc(sd_ready, 1)
                for t in range(T):
                    act.wait_ge(y_ready, t + 1)
                    if t >= 1:
                        act.wait_ge(ms_ready, t)
                    act.activation(square[:, :], Y[:, t, :], ACT.Square, accum_out=ms[:, t:t + 1]).then_inc(ms_ready, 1)
                act.wait_ge(ve_ready, 2)
                act.activation(sd[:, :], ve[:, :], ACT.Sqrt).then_inc(sd_ready, 1)
                for t in range(T):
                    act.wait_ge(t_full, t + 1)
                    act.activation(xgT[:, :, t * P:(t + 1) * P],
                                   ps_t[t % 2][:, :].rearrange("p (k q) -> p k q", q=P), ACT.Copy).then_inc(t_ready, 1)

            @block.vector
            def _(dve):
                lk = Link(dve, link)
                lk(dve.reciprocal(rden[:, :, :], part[:, :, :, DH]))
                dve.wait_ge(row_in, 32)

                def normalised(t):
                    if t >= 2:
                        dve.wait_ge(hT_full, t - 1)
                    dve.tensor_tensor(hn[t % 2][:, :].rearrange("p (h d) -> p h d", h=H), part[:, t, :, 0:DH],
                                      rden[:, t, :, None].to_broadcast([P, H, DH]), ALU.mult).then_inc(hn_ready, 1)

                def residual(t):
                    dve.wait_ge(exp_ready, t + 1)
                    if t % 4 == 0:
                        dve.wait_ge(x_in[t // 4], 16)
                    lk(dve.scalar_tensor_tensor(v[t % 2][:, :], v[t % 2][:, :], 0.0, low[t % 2][:, :], ALU.max, ALU.add))
                    lk(dve.scalar_tensor_tensor(X1[:, t, :], v[t % 2][:, :], -1.0, X1[:, t, :], ALU.add, ALU.add))
                    dve.bn_stats(stats[:, t, :], X1[:, t, :]).then_inc(x1_ready, 1)

                normalised(0)
                for t in range(T):
                    if t + 1 < T:
                        normalised(t + 1)
                    if t >= 1:
                        residual(t - 1)
                    dve.wait_ge(full, t + 1)
                    lk(dve.tensor_tensor(v[t % 2][:, :], ps_s[t % 2][:, :], brow[:, :], ALU.add))
                    dve.tensor_scalar(low[t % 2][:, :], v[t % 2][:, :], 0.0, None, ALU.min).then_inc(low_ready, 1)
                residual(T - 1)
                dve.wait_ge(x1_ready, T)
                for t in range(T):
                    last = dve.bn_aggr(mv[:, t, :], stats[:, t, :])
                lk(last)
                lk(dve.tensor_scalar(ve[:, :], mv[:, :, 1], LN_EPS, None, ALU.add))
                dve.sem_inc(ve_ready, 1)
                dve.wait_ge(sd_ready, 1)
                root_of_inverse(dve, lk, rstd, sd, ve)
                for t in range(T):
                    dve.tensor_scalar(Y[:, t, :], X1[:, t, :], mv[:, t, 0:1], rstd[:, t:t + 1],
                                      ALU.subtract, ALU.mult).then_inc(y_ready, 1)
                dve.wait_ge(ms_ready, T)
                lk(dve.tensor_scalar(ve[:, :], ms[:, :], 1.0 / D, RMS_EPS, ALU.mult, ALU.add))
                dve.sem_inc(ve_ready, 1)
                dve.wait_ge(sd_ready, 2)
                root_of_inverse(dve, lk, rms, sd, ve)
                for t in range(T):
                    dve.scalar_tensor_tensor(Y[:, t, :], Y[:, t, :], rms[:, t:t + 1], grow[:, :],
                                             ALU.mult, ALU.mult).then_inc(xg_ready, 1)

            @block.tensor
            def _(pe):
                def product(t):
                    pe.wait_ge(hT_ready, t + 1)
                    if t == 0:
                        pe.wait_ge(w_in, 16)
                    if t >= 2:
                        pe.wait_ge(low_ready, t - 1)
                    for k in range(KD):
                        mm = pe.matmul(ps_s[t % 2][:, :], hT[t % 2][:, k, :], W[:, k, :],
                                       start=(k == 0), stop=(k == KD - 1))
                    mm.then_inc(full, 1)

                for t in range(T):
                    pe.wait_ge(hn_ready, t + 1)
                    if t >= 2:
                        pe.wait_ge(hT_ready, t - 1)
                    for k in range(KD):
                        mm = pe.transpose(ps_t[t % 2][:, k * P:(k + 1) * P], hn[t % 2][:, k * P:(k + 1) * P], ident[:, :])
                    mm.then_inc(hT_full, 1)
                    if t >= 1:
                        product(t - 1)
                product(T - 1)
                for t in range(T):
                    pe.wait_ge(xg_ready, t + 1)
                    if t >= 2:
                        pe.wait_ge(t_ready, t - 1)
                    for k in range(KD):
                        mm = pe.transpose(ps_t[t % 2][:, k * P:(k + 1) * P], Y[:, t, k * P:(k + 1) * P], ident[:, :])
                    mm.then_inc(t_full, 1)


EXPERTS, FFN, TOP, CAP = 8, 1024, 2, 640
ROWS = 3 * DH
NC = N // BANK


def stage_qkv(nc, sem, keep, w_qkv, cos, sin, parts_dram):
    xgT, V = keep["xgT"], keep["V"]
    with Stage(nc, "q") as st:
        W = st.sb("w", [P, KD, 3 * D])
        C, S = st.sb("cos", [P, N]), st.sb("sin", [P, N])
        raw = [st.sb(f"raw{i}", [P, BANK]) for i in range(2)]
        swap = [st.sb(f"swap{i}", [P, BANK]) for i in range(2)]
        turn = [st.sb(f"turn{i}", [P, BANK]) for i in range(2)]
        hi = [st.sb(f"hi{i}", [P, BANK], F32R) for i in range(2)]
        lo = [st.sb(f"lo{i}", [P, BANK], F32R) for i in range(2)]
        ps = [st.ps(f"p{i}", [P, BANK]) for i in range(4)]
        w_in = [sem(f"q_w_in{i}") for i in range(3)]
        t_in = sem("q_t_in")
        link, full, v_done, raw_ready, cos_done, parts_ready = (
            sem("q_" + n) for n in ("link", "full", "v", "raw", "cosd", "parts"))
        sent = [sem(f"q_sent{i}") for i in range(2)]
        jobs = [(m, g, c) for m in range(2) for g in range(KD) for c in range(NC)]
        with nc.Block() as block:

            @block.sync
            def _(sp):
                wv = w_qkv.rearrange("(k p) n -> p k n", p=P)
                for m in (2, 0, 1):
                    sp.dma_start(W[:, :, m * D:(m + 1) * D], wv[:, :, m * D:(m + 1) * D]).then_inc(w_in[m], 16)
                sp.dma_start(C[:, :], cos).then_inc(t_in, 16)
                sp.dma_start(S[:, :], sin).then_inc(t_in, 16)
                for n, (m, g, c) in enumerate(jobs):
                    sp.wait_ge(parts_ready, n + 1)
                    for z, part in enumerate((hi, lo)):
                        sp.dma_start(parts_dram[2 * m + z, g * P:(g + 1) * P, c * BANK:(c + 1) * BANK],
                                     part[n % 2][:, :].bitcast(F32)).then_inc(sent[n % 2], 16)
                for r in range(2):
                    sp.wait_ge(sent[r], 32 * len(jobs) // 2)

            @block.tensor
            def _(pe):
                pe.wait_ge(w_in[2], 16)
                for t in range(T):
                    if t >= 4:
                        pe.wait_ge(v_done, t - 3)
                    for k in range(KD):
                        mm = pe.matmul(ps[t % 4][:, :], xgT[:, k, t * P:(t + 1) * P], W[:, k, 2 * D:3 * D],
                                       start=(k == 0), stop=(k == KD - 1))
                    mm.then_inc(full, 1)
                for n, (m, g, c) in enumerate(jobs):
                    if n == 0:
                        pe.wait_ge(w_in[0], 16)
                        pe.wait_ge(w_in[1], 16)
                    if n < 4:
                        pe.wait_ge(v_done, T - 3 + n)
                    else:
                        pe.wait_ge(raw_ready, n - 3)
                    for k in range(KD):
                        mm = pe.matmul(ps[n % 4][:, :], W[:, k, m * D + g * P:m * D + (g + 1) * P],
                                       xgT[:, k, c * BANK:(c + 1) * BANK], start=(k == 0), stop=(k == KD - 1))
                    mm.then_inc(full, 1)

            @block.scalar
            def _(act):
                for t in range(T):
                    act.wait_ge(full, t + 1)
                    act.activation(V[:, t, :], ps[t % 4][:, :], ACT.Copy).then_inc(v_done, 1)
                for n in range(len(jobs)):
                    act.wait_ge(full, T + n + 1)
                    if n >= 2:
                        act.wait_ge(cos_done, n - 1)
                        act.wait_ge(parts_ready, n - 1)
                    act.activation(raw[n % 2][:, :], ps[n % 4][:, :], ACT.Copy).then_inc(raw_ready, 1)

            @block.gpsimd
            def _(pool):
                pool.wait_ge(t_in, 32)
                for n, (m, g, c) in enumerate(jobs):
                    pool.wait_ge(raw_ready, n + 1)
                    if n >= 2:
                        pool.wait_ge(parts_ready, n - 1)
                    pool.tensor_tensor(turn[n % 2][:, :], raw[n % 2][:, :], C[:, c * BANK:(c + 1) * BANK],
                                       ALU.mult).then_inc(cos_done, 1)

            @block.vector
            def _(dve):
                lk = Link(dve, link)
                dve.wait_ge(t_in, 32)
                for n, (m, g, c) in enumerate(jobs):
                    r = n % 2
                    dve.wait_ge(raw_ready, n + 1)
                    lk(dve.stream_shuffle(swap[r][:, :], raw[r][:, :], [d ^ 1 for d in range(32)]))
                    lk(dve.tensor_tensor(swap[r][:, :], swap[r][:, :], S[:, c * BANK:(c + 1) * BANK], ALU.mult))
                    dve.wait_ge(cos_done, n + 1)
                    lk(dve.tensor_tensor(swap[r][:, :], swap[r][:, :], turn[r][:, :], ALU.add))
                    if n >= 2:
                        dve.wait_ge(sent[r], 32 * (n // 2))
                    lk(dve.tensor_copy(hi[r][:, :], swap[r][:, :]))
                    dve.tensor_tensor(lo[r][:, :], swap[r][:, :], hi[r][:, :].bitcast(F32), ALU.subtract).then_inc(parts_ready, 1)


def stage_attention(nc, sem, keep, parts_dram, o_dram):
    V, ident, ident_b = keep["V"], keep["ident"], keep["ident_b"]
    SCALE = float(DH) ** -0.5
    BIG = -1e30
    STEPS = []
    for c in range(NC):
        STEPS += [(c, kt, 0, BANK) for kt in range(0, 4 * c, 2)]
        STEPS += [(c, 4 * c, 0, BANK), (c, 4 * c + 2, 2 * P, 2 * P)]
    NS = len(STEPS)
    END = {c: max(s for s in range(NS) if STEPS[s][0] == c) for c in range(NC)}
    PIECES = [(hh, t, ch, BANK if ch < t // 4 else (t % 4 + 1) * P)
              for hh in range(2) for t in range(T) for ch in range(t // 4 + 1)]
    NP = len(PIECES)
    FROM, TO = 3, 16
    share = [0] * NS
    for p in range(NP):
        share[FROM + p * (TO - FROM) // NP] += 1
    GAPS = 4
    K1 = ROWS + 1
    OUT = DH + 1
    with Stage(nc, "t") as st:
        Q = [[st.sb(f"Q{r}{hh}", [P, N], F32R) for hh in range(2)] for r in range(2)]
        K = [[st.sb(f"K{r}{hh}", [P, N], F32R) for hh in range(2)] for r in range(2)]
        v = [st.sb(f"v{r}", [P, T, 2, DH]) for r in range(2)]
        E = [[st.sb(f"E{s}{hh}", [P, 2, BANK]) for hh in range(2)] for s in range(2)]
        ones = st.sb("ones", [P, DH])
        triq, trik = st.sb("triq", [P, P], BF16), st.sb("trik", [P, 2 * P], BF16)
        rm = st.sb("rm", [P, 2, T, NC])
        m = st.sb("m", [P, 2 * T])
        mT = st.sb("mT", [2 * T, P], F32R)
        out = [st.sb(f"out{i}", [P, BANK]) for i in range(2)]
        ps_s = [st.ps(f"s{hh}", [P, 2 * BANK]) for hh in range(2)]
        ps_o = [st.ps(f"o{i}", [P, BANK]) for i in range(2)]
        ps_m = [st.ps(f"m{i}", [P, BANK]) for i in range(2)]
        stack_in = [sem(f"t_stack_in{r}") for r in range(2)]
        stack_free = [sem(f"t_stack_free{r}") for r in range(2)]
        v_in = [sem(f"t_v_in{r}") for r in range(2)]
        v_free = [sem(f"t_v_free{r}") for r in range(2)]
        m_in = [sem(f"t_m_in{r}") for r in range(2)]
        s_full = [sem(f"t_s_full{hh}") for hh in range(2)]
        exp_done = [sem(f"t_exp{hh}") for hh in range(2)]
        pv_done, o_copied, piece_full, piece_read, m_ready, mT_full, mT_ready, setup, link = (
            sem("t_" + n) for n in ("pv", "o_copied", "pf", "pr", "m_ready", "mTf", "mTr", "setup", "link"))
        o_sent = [sem(f"t_o_sent{i}") for i in range(2)]
        LAST = H // 4 - 1
        with nc.Block() as block:

            @block.sync
            def _(sp):
                def load(j, r):
                    for hh in range(2):
                        row = (j * 4 + 2 * r + hh) * DH
                        for dst, order in ((Q[r][hh], (0, 0, 1)), (K[r][hh], (2, 3, 2))):
                            for b, part in enumerate(order):
                                sp.dma_start(dst[b * DH:(b + 1) * DH, :].bitcast(F32),
                                             parts_dram[part, ds(row, DH), :]).then_inc(stack_in[r], 16)

                def store(j, r, c):
                    sp.wait_ge(o_copied, j * 2 * NC + r * NC + c + 3)
                    for hh in range(2):
                        row = (j * 4 + 2 * r + hh) * OUT
                        sp.dma_start(o_dram[ds(row, OUT), c * BANK:(c + 1) * BANK],
                                     out[c % 2][64 * hh:64 * hh + OUT, :]).then_inc(o_sent[c % 2], 16)

                def maxima(j, r):
                    sp.wait_ge(mT_ready, j * 2 + r + 1)
                    for hh in range(2):
                        sp.dma_start(Q[r][hh][ROWS:K1, :].bitcast(F32).rearrange("p (t q) -> p t q", t=T),
                                     mT[hh * T:(hh + 1) * T, :].bitcast(F32)).then_inc(m_in[r], 16)

                def main(j, r, following):
                    for c in range(NC):
                        if c == NC - 1:
                            if following is not None:
                                maxima(*following)
                            if j is not LAST:
                                sp.wait_ge(stack_free[r], j + 1)
                                load(j + 1, r)
                        store(j, r, c)

                load(0, 0)
                load(0, 1)
                maxima(0, 0)
                with sp.Fori(0, LAST) as j:
                    main(j, 0, (j, 1))
                    main(j, 1, (j + 1, 0))
                main(LAST, 0, (LAST, 1))
                main(LAST, 1, None)
                for i in range(2):
                    sp.wait_ge(o_sent[i], 32 + 32 * (H // 2) * NC // 2)

            @block.gpsimd
            def _(pool):
                pool.memset(triq[:, :], 0.0).then_inc(setup, 1)
                pool.memset(trik[:, 0:P], BIG).then_inc(setup, 1)
                pool.memset(trik[:, P:2 * P], 0.0).then_inc(setup, 1)
                pool.memset(ones[:, :], 1.0).then_inc(setup, 1)
                pool.wait_ge(setup, 8)
                pool.affine_select(out=triq[:, :], in_=triq[:, :], compare_op=ALU.is_ge, fill=BIG,
                                   base=0, pattern=[[-1, P]], channel_multiplier=1).then_inc(setup, 1)
                pool.affine_select(out=trik[:, P:2 * P], in_=trik[:, P:2 * P], compare_op=ALU.is_ge, fill=BIG,
                                   base=0, pattern=[[1, P]], channel_multiplier=-1).then_inc(setup, 1)
                for r in range(2):
                    pool.sem_inc(v_free[r], 1)
                with pool.Fori(0, H // 4) as j:
                    for r in range(2):
                        pool.wait_ge(v_free[r], j + 1)
                        col = (j * 4 + 2 * r) * DH
                        pool.tensor_copy(v[r][:, :, :, :].rearrange("p t h d -> p t (h d)"),
                                         V[:, :, ds(col, 2 * DH)]).then_inc(v_in[r], 1)

            @block.scalar
            def _(act):
                for hh in range(2):
                    act.sem_inc(exp_done[hh], 1)
                def main(j, r):
                    base = j * (2 * NS) + r * NS
                    for s, (c, kt, off, w) in enumerate(STEPS):
                        for hh in range(2):
                            act.wait_ge(s_full[hh], base + s + 1)
                            act.wait_ge(pv_done, base + s + 1)
                            act.activation(E[s % 2][hh][:, :, 0:w],
                                           ps_s[hh][:, :].rearrange("p (b n) -> p b n", b=2)[:, :, 0:w],
                                           ACT.Exp, scale=SCALE).then_inc(exp_done[hh], 1)

                with act.Fori(0, H // 4) as j:
                    for r in range(2):
                        main(j, r)

            @block.vector
            def _(dve):
                lk = Link(dve, link)
                for r in range(2):
                    for hh in range(2):
                        dve.memset(K[r][hh][ROWS:K1, :].bitcast(F32), 1.0).then_inc(setup, 1)
                lk(dve.memset(rm[:, :, :, :], -3e38))
                dve.sem_inc(piece_read, 2)
                dve.sem_inc(o_copied, 2)
                for i in range(2):
                    dve.sem_inc(o_sent[i], 32)

                def copy(j, r, c):
                    i = c % 2
                    dve.wait_ge(pv_done, j * (2 * NS) + r * NS + END[c] + 3)
                    dve.wait_ge(o_sent[i], j * (32 * NC) + r * (16 * NC) + (c // 2) * 32 + 32)
                    dve.tensor_copy(out[i][:, :], ps_o[i][:, :]).then_inc(o_copied, 1)

                def piece(j, r, p):
                    hh, t, ch, w = PIECES[p]
                    dve.wait_ge(piece_full, j * (2 * NP) + r * NP + p + 1)
                    dve.tensor_reduce(rm[:, hh, t, ch:ch + 1], ps_m[p % 2][:, 0:w], AX, ALU.max).then_inc(piece_read, 1)

                def maxima(j, r, first=False):
                    dve.wait_ge(piece_read, j * (2 * NP) + r * NP + NP + 2)
                    lk(dve.tensor_reduce(m[:, :], rm[:, :, :, :].rearrange("p h t c -> p (h t) c"), AX, ALU.max))
                    lk(dve.tensor_scalar(m[:, :], m[:, :], -1.0, None, ALU.mult))
                    dve.sem_inc(m_ready, 1)
                    dve.wait_ge(mT_full, j * 2 + r + 1)
                    if not first:
                        dve.wait_ge(m_in[1 - r], (j * 32 + 32) if r else (j * 32))
                    lk(dve.tensor_copy(mT[:, :], ps_m[0][0:2 * T, 0:P]))
                    dve.sem_inc(mT_ready, 1)

                def main(j, r, following):
                    p = 0
                    for s, (c, kt, off, w) in enumerate(STEPS):
                        if following is not None:
                            for _ in range(share[s]):
                                piece(*following, p)
                                p += 1
                            if s == TO:
                                maxima(*following)
                        if s == END[c]:
                            copy(j, r, c)

                for p in range(NP):
                    piece(0, 0, p)
                maxima(0, 0, first=True)
                with dve.Fori(0, LAST) as j:
                    lk.restart()
                    main(j, 0, (j, 1))
                    main(j, 1, (j + 1, 0))
                lk.restart()
                main(LAST, 0, (LAST, 1))
                main(LAST, 1, None)

            @block.tensor
            def _(pe):
                pe.sem_inc(pv_done, 2)

                def piece(j, r, p):
                    hh, t, ch, w = PIECES[p]
                    if p == 0:
                        pe.wait_ge(stack_in[r], j * 192 + 192)
                    pe.wait_ge(piece_read, j * (2 * NP) + r * NP + p + 1)
                    diag = ch == t // 4
                    mm = pe.matmul(ps_m[p % 2][:, 0:w], Q[r][hh][0:ROWS, t * P:(t + 1) * P],
                                   K[r][hh][0:ROWS, ch * BANK:ch * BANK + w], start=True, stop=not diag)
                    if diag:
                        mm = pe.matmul(ps_m[p % 2][:, w - P:w], ident_b[:, :], triq[:, :], start=False, stop=True)
                    mm.then_inc(piece_full, 1)

                def maxima(j, r):
                    pe.wait_ge(m_ready, j * 2 + r + 1)
                    pe.transpose(ps_m[0][0:2 * T, 0:P], m[:, :], ident[:, :]).then_inc(mT_full, 1)

                def scores(j, r, s, hh):
                    c, kt, off, w = STEPS[s]
                    base = j * (2 * NS) + r * NS
                    if s == 0 and hh == 0:
                        pe.wait_ge(m_in[r], j * 32 + 32)
                    pe.wait_ge(exp_done[hh], base + s + 1)
                    q0 = c * BANK + off
                    diag = kt >= 4 * c
                    for b in range(2):
                        o = b * BANK
                        mm = pe.matmul(ps_s[hh][:, o:o + w], K[r][hh][0:K1, (kt + b) * P:(kt + b + 1) * P],
                                       Q[r][hh][0:K1, q0:q0 + w], start=True, stop=not diag)
                        if diag and b == 0:
                            mm = pe.matmul(ps_s[hh][:, o:o + P], ident_b[:, :], trik[:, P:2 * P], start=False, stop=True)
                        if diag and b == 1:
                            mm = pe.matmul(ps_s[hh][:, o:o + 2 * P], ident_b[:, :], trik[:, :], start=False, stop=True)
                    mm.then_inc(s_full[hh], 1)

                def values(j, r, s, b):
                    c, kt, off, w = STEPS[s]
                    base = j * (2 * NS) + r * NS
                    if s == 0:
                        pe.wait_ge(v_in[r], j + 1)
                    if kt + b == 0:
                        pe.wait_ge(o_copied, j * (2 * NC) + r * NC + c + 1)
                    for hh in range(2):
                        pe.wait_ge(exp_done[hh], base + s + 2)
                    for hh in range(2):
                        for z, lhs in enumerate((v[r][:, kt + b, hh, :], ones[:, :])):
                            g = 64 * hh + DH * z
                            mm = pe.matmul(ps_o[c % 2][g:g + DH, off:off + w], lhs, E[s % 2][hh][:, b, 0:w],
                                           start=(kt + b == 0), stop=(kt + b == 4 * c + 3))
                    if b == 1:
                        mm.then_inc(pv_done, 1)

                def main(j, r, following):
                    p = 0
                    for s in range(NS):
                        if s == NS - 1:
                            for hh in range(2):
                                pe.wait_ge(s_full[hh], j * (2 * NS) + r * NS + NS)
                            pe.sem_inc(stack_free[r], 1)
                        n = share[s] if following is not None else 0
                        for gap in range(GAPS):
                            if gap >= 2:
                                values(j, r, s, gap - 2)
                            elif s + 1 < NS:
                                scores(j, r, s + 1, gap)
                            elif following is not None:
                                scores(*following, 0, gap)
                            for _ in range((n + gap) // GAPS):
                                piece(*following, p)
                                p += 1
                        if following is not None and s == TO:
                            maxima(*following)
                    pe.wait_ge(pv_done, j * (2 * NS) + r * NS + NS + 2)
                    pe.sem_inc(v_free[r], 1)

                pe.wait_ge(setup, 10)
                for p in range(NP):
                    piece(0, 0, p)
                maxima(0, 0)
                for hh in range(2):
                    scores(0, 0, 0, hh)
                with pe.Fori(0, LAST) as j:
                    main(j, 0, (j, 1))
                    main(j, 1, (j + 1, 0))
                main(LAST, 0, (LAST, 1))
                main(LAST, 1, None)


def stage_router(nc, sem, keep, w_o, g2, w_router, o_dram, rec_dram, res_dram):
    X1, Z, mv, rstd, prob, ident = (keep[n] for n in ("X1", "Z", "mv", "rstd", "prob", "ident"))
    with Stage(nc, "r") as st:
        W, Wr = st.sb("w", [P, KD, D]), st.sb("wr", [P, KD, EXPERTS])
        oT = st.sb("oT", [P, KD, N])
        share = st.sb("share", [P, H * N // P])
        by = [st.sb(f"by{c}", [P, KD, BANK]) for c in range(2)]
        grow = st.sb("grow", [P, D])
        y0 = [st.sb(f"y0{i}", [P, D]) for i in range(2)]
        square = st.sb("square", [P, D])
        zT = [st.sb(f"zT{i}", [P, KD, P]) for i in range(2)]
        ms, ve, sd, rms = (st.sb(n, [P, T]) for n in ("ms", "ve", "sd", "rms"))
        lg = st.sb("lg", [P, T, EXPERTS])
        top, total = st.sb("top", [P, T, 1]), st.sb("total", [P, T, 1])
        ps = [st.ps(f"p{i}", [P, BANK]) for i in range(4)]
        ps_t = [st.ps(f"t{i}", [P, BANK]) for i in range(2)]
        ps_l = st.ps("l", [P, BANK])
        o_in = [sem(f"r_o_in{c}") for c in range(NC)]
        by_in = [sem(f"r_by_in{c}") for c in range(2)]
        den_in, share_ready, share_out, o_ready = (sem("r_" + n) for n in ("den_in", "share", "share_out", "o_ready"))
        w_in, link, full, y_ready, ms_ready, ve_ready, sd_ready, z_ready, zT_full, zT_ready = (
            sem("r_" + n) for n in ("w_in", "link", "full", "y", "ms", "ve", "sd", "z", "zTf", "zTr"))
        lg_full, res_ready, res_out, shifted, exp_done = (sem("r_" + n) for n in ("lg", "res", "res_out", "shift", "exp"))
        with nc.Block() as block:

            @block.sync
            def _(sp):
                ov = o_dram.rearrange("(h d) n -> h d n", d=DH + 1)
                sp.dma_start(share[:, :], ov[:, DH, :].rearrange("h (b q) -> h b q", b=P // H)).then_inc(den_in, 16)
                ok = ov.rearrange("(k g) d n -> g d k n", k=KD)
                for c in range(NC):
                    for g in range(P // DH):
                        sp.dma_start(oT[g * DH:(g + 1) * DH, :, c * BANK:(c + 1) * BANK],
                                     ok[g, 0:DH, :, c * BANK:(c + 1) * BANK]).then_inc(o_in[c], 16)
                sp.dma_start(W[:, :, :], w_o.rearrange("(k p) n -> p k n", p=P)).then_inc(w_in, 16)
                sp.dma_start(grow[:, :], g2.partition_broadcast(P)).then_inc(w_in, 16)
                sp.dma_start(Wr[:, :, :], w_router.rearrange("(k p) n -> p k n", p=P)).then_inc(w_in, 16)
                for c in range(4):
                    sp.wait_ge(res_ready, 4 * c + 4)
                    sp.dma_start(res_dram.rearrange("(t p) d -> p t d", p=P)[:, 4 * c:4 * c + 4, :],
                                 X1[:, 4 * c:4 * c + 4, :]).then_inc(res_out, 16)
                sp.wait_ge(res_out, 64)

            @block.gpsimd
            def _(pool):
                pool.wait_ge(share_ready, 1)
                pool.dma_start(rec_dram.rearrange("h (b q) -> (h b) q", b=P // H), share[:, :]).then_inc(share_out, 16)
                pool.wait_ge(share_out, 16)
                rv = rec_dram.rearrange("(k g) n -> g k n", k=KD)
                for c in range(NC):
                    if c >= 2:
                        pool.wait_ge(o_ready, c - 1)
                    for g in range(P // DH):
                        pool.dma_start(by[c % 2][g * DH:(g + 1) * DH, :, :],
                                       rv[g, :, c * BANK:(c + 1) * BANK].partition_broadcast(DH)).then_inc(by_in[c % 2], 16)
                for t in range(T):
                    pool.wait_ge(y_ready, t + 1)
                    pool.tensor_tensor(X1[:, t, :], X1[:, t, :], Z[:, t, :], ALU.add).then_inc(res_ready, 1)

            @block.tensor
            def _(pe):
                pe.wait_ge(w_in, 48)
                for t in range(T):
                    if t % 4 == 0:
                        pe.wait_ge(o_ready, t // 4 + 1)
                    if t >= 4:
                        pe.wait_ge(y_ready, t - 3)
                    for k in range(KD):
                        mm = pe.matmul(ps[t % 4][:, :], oT[:, k, t * P:(t + 1) * P], W[:, k, :],
                                       start=(k == 0), stop=(k == KD - 1))
                    mm.then_inc(full, 1)

                def logits(t):
                    pe.wait_ge(zT_ready, t + 1)
                    for k in range(KD):
                        mm = pe.matmul(ps_l[:, t * EXPERTS:(t + 1) * EXPERTS], zT[t % 2][:, k, :], Wr[:, k, :],
                                       start=(k == 0), stop=(k == KD - 1))
                    mm.then_inc(lg_full, 1)

                for t in range(T):
                    pe.wait_ge(z_ready, t + 1)
                    if t >= 2:
                        pe.wait_ge(zT_ready, t - 1)
                    for k in range(KD):
                        mm = pe.transpose(ps_t[t % 2][:, k * P:(k + 1) * P], Z[:, t, k * P:(k + 1) * P], ident[:, :])
                    mm.then_inc(zT_full, 1)
                    if t >= 1:
                        logits(t - 1)
                logits(T - 1)

            @block.scalar
            def _(act):
                for t in range(T):
                    act.wait_ge(y_ready, t + 1)
                    if t >= 1:
                        act.wait_ge(ms_ready, t)
                    act.activation(square[:, :], Z[:, t, :], ACT.Square, accum_out=ms[:, t:t + 1]).then_inc(ms_ready, 1)
                act.wait_ge(ve_ready, 1)
                act.activation(sd[:, :], ve[:, :], ACT.Sqrt).then_inc(sd_ready, 1)
                for t in range(T):
                    act.wait_ge(zT_full, t + 1)
                    if t >= 2:
                        act.wait_ge(lg_full, t - 1)
                    act.activation(zT[t % 2][:, :, :], ps_t[t % 2][:, :].rearrange("p (k q) -> p k q", q=P),
                                   ACT.Copy).then_inc(zT_ready, 1)
                act.wait_ge(shifted, 1)
                act.activation(lg[:, :, :], lg[:, :, :], ACT.Exp).then_inc(exp_done, 1)

            @block.vector
            def _(dve):
                lk = Link(dve, link)
                dve.wait_ge(den_in, 16)
                dve.reciprocal(share[:, :], share[:, :]).then_inc(share_ready, 1)
                for t in range(T):
                    if t % 4 == 0:
                        c = t // 4
                        dve.wait_ge(o_in[c], 16 * (P // DH))
                        dve.wait_ge(by_in[c % 2], 16 * (P // DH) * (c // 2 + 1))
                        part = oT[:, :, c * BANK:(c + 1) * BANK]
                        dve.tensor_tensor(part, part, by[c % 2][:, :, :], ALU.mult).then_inc(o_ready, 1)
                    lk(dve.tensor_scalar(y0[t % 2][:, :], X1[:, t, :], mv[:, t, 0:1], rstd[:, t:t + 1],
                                         ALU.subtract, ALU.mult))
                    dve.wait_ge(full, t + 1)
                    dve.tensor_tensor(Z[:, t, :], y0[t % 2][:, :], ps[t % 4][:, :], ALU.add).then_inc(y_ready, 1)
                dve.wait_ge(ms_ready, T)
                lk(dve.tensor_scalar(ve[:, :], ms[:, :], 1.0 / D, RMS_EPS, ALU.mult, ALU.add))
                dve.sem_inc(ve_ready, 1)
                dve.wait_ge(sd_ready, 1)
                root_of_inverse(dve, lk, rms, sd, ve)
                dve.wait_ge(w_in, 48)
                for t in range(T):
                    dve.wait_ge(res_ready, t + 1)
                    dve.scalar_tensor_tensor(Z[:, t, :], Z[:, t, :], rms[:, t:t + 1], grow[:, :],
                                             ALU.mult, ALU.mult).then_inc(z_ready, 1)
                dve.wait_ge(lg_full, T)
                pl = ps_l[:, 0:T * EXPERTS].rearrange("p (t e) -> p t e", e=EXPERTS)
                lk(dve.tensor_reduce(top[:, :, :], pl, AX, ALU.max))
                lk(dve.tensor_tensor(lg[:, :, :], pl, top[:, :, :].to_broadcast([P, T, EXPERTS]), ALU.subtract))
                dve.sem_inc(shifted, 1)
                dve.wait_ge(exp_done, 1)
                lk(dve.tensor_reduce(total[:, :, :], lg[:, :, :], AX, ALU.add))
                lk(dve.reciprocal(total[:, :, :], total[:, :, :]))
                lk(dve.tensor_tensor(prob[:, :, :], lg[:, :, :], total[:, :, :].to_broadcast([P, T, EXPERTS]), ALU.mult))


FAR = 1 << 20


def stage_slots(nc, sem, keep, xe_dram):
    Z, prob, gate, place = (keep[n] for n in ("Z", "prob", "gate", "place"))
    E = EXPERTS
    with Stage(nc, "s") as st:
        above = st.sb("above", [P, T, E, E])
        equal = st.sb("equal", [P, T, E, E])
        lower = st.sb("lower", [P, E, E])
        rank, G, sel, over, tie, tmp, slot = (st.sb(n, [P, T, E]) for n in ("rank", "G", "sel", "over", "tie", "tmp", "slot"))
        keptb, hit = st.sb("keptb", [P, T, E], BF16), st.sb("hit", [P, T, E], BF16)
        thr, cand = st.sb("thr", [P, E], I32), st.sb("cand", [P, E], I32)
        more = st.sb("more", [P, E], I32)
        room = st.sb("room", [P, E])
        first = st.sb("first", [P, E])
        onesb, before = st.sb("onesb", [P, P], BF16), st.sb("before", [P, P], BF16)
        choice = st.sb("choice", [P, T, E])
        kept = st.sb("kept", [P, T])
        dest = st.sb("dest", [P, T])
        index = st.sb("index", [P, 2, T], U32)
        ps_c = st.ps("c", [P, BANK])
        ps_p = st.ps("p", [P, BANK])
        setup, link, hit_ready, counted, kept_ready, placed, index_ready, scattered = (
            sem("s_" + n) for n in ("setup", "link", "hit", "counted", "kept", "placed", "index", "scattered"))
        BITS = list(range(29, -1, -1))
        flat = lambda a: a[:, :, :].rearrange("p t e -> p (t e)")
        with nc.Block() as block:

            @block.gpsimd
            def _(pool):
                pool.memset(lower[:, :, :], 1.0).then_inc(setup, 1)
                pool.memset(onesb[:, :], 1.0).then_inc(setup, 1)
                pool.memset(before[:, :], 1.0).then_inc(setup, 1)
                for e in range(E):
                    pool.memset(first[:, e:e + 1], float(e * CAP)).then_inc(setup, 1)
                pool.wait_ge(setup, 3 + E)
                pool.affine_select(out=lower[:, :, :], in_=lower[:, :, :], compare_op=ALU.is_gt, fill=0.0,
                                   base=0, pattern=[[1, E], [-1, E]], channel_multiplier=0).then_inc(setup, 1)
                pool.affine_select(out=before[:, :], in_=before[:, :], compare_op=ALU.is_gt, fill=0.0,
                                   base=0, pattern=[[1, P]], channel_multiplier=-1).then_inc(setup, 1)
                for c in range(TOP):
                    pool.wait_ge(index_ready, c + 1)
                    for t in range(T):
                        pool.indirect_dma_start(out=xe_dram, out_offset=bass.IndirectOffsetOnAxis(ap=index[:, c, t:t + 1], axis=0),
                                                in_=Z[:, t, :], in_offset=None, bounds_check=E * CAP - 1,
                                                oob_is_err=False).then_inc(scattered, 16)
                pool.wait_ge(scattered, 16 * TOP * T)

            @block.vector
            def _(dve):
                lk = Link(dve, link)
                dve.wait_ge(setup, 5 + E)
                mine = prob[:, :, :, None].to_broadcast([P, T, E, E])
                other = prob[:, :, None, :].to_broadcast([P, T, E, E])
                dve.tensor_tensor(above[:, :, :, :], other, mine, ALU.is_gt)
                lk(dve.tensor_tensor(equal[:, :, :, :], other, mine, ALU.is_equal))
                lk(dve.tensor_tensor(equal[:, :, :, :], equal[:, :, :, :],
                                     lower[:, None, :, :].to_broadcast([P, T, E, E]), ALU.mult))
                lk(dve.tensor_tensor(above[:, :, :, :], above[:, :, :, :], equal[:, :, :, :], ALU.add))
                lk(dve.tensor_reduce(rank[:, :, :], above[:, :, :, :], AX, ALU.add))
                lk(dve.tensor_scalar(sel[:, :, :], rank[:, :, :], TOP - 0.5, None, ALU.is_lt))
                lk(dve.tensor_tensor(G[:, :, :], prob[:, :, :], sel[:, :, :], ALU.mult))
                lk(dve.memset(thr[:, :], 0))
                for n, bit in enumerate(BITS):
                    lk(dve.tensor_scalar(cand[:, :], thr[:, :], 1 << bit, None, ALU.bitwise_or))
                    dve.tensor_tensor(hit[:, :, :], G[:, :, :],
                                      cand[:, None, :].bitcast(F32).to_broadcast([P, T, E]), ALU.is_ge).then_inc(hit_ready, 1)
                    dve.wait_ge(counted, n + 1)
                    lk(dve.tensor_reduce(room[:, :], ps_c[:, 0:T * E].rearrange("p (t e) -> p e t", e=E), AX, ALU.add))
                    lk(dve.tensor_scalar(more[:, :], room[:, :], CAP - 0.5, None, ALU.is_gt))
                    lk(dve.copy_predicated(thr[:, :], more[:, :], cand[:, :]))
                line = thr[:, None, :].bitcast(F32).to_broadcast([P, T, E])
                dve.tensor_tensor(over[:, :, :], G[:, :, :], line, ALU.is_gt)
                dve.tensor_tensor(tie[:, :, :], G[:, :, :], line, ALU.is_equal)
                lk(dve.tensor_tensor(hit[:, :, :], G[:, :, :], line, ALU.is_gt))
                dve.sem_inc(hit_ready, 1)
                lk(dve.tensor_tensor(tie[:, :, :], tie[:, :, :], sel[:, :, :], ALU.mult))
                lk(dve.tensor_copy(keptb[:, :, :], tie[:, :, :]))
                dve.sem_inc(kept_ready, 1)
                dve.wait_ge(counted, len(BITS) + 1)
                lk(dve.tensor_reduce(room[:, :], ps_c[:, 0:T * E].rearrange("p (t e) -> p e t", e=E), AX, ALU.add))
                lk(dve.tensor_scalar(room[:, :], room[:, :], -1.0, float(CAP), ALU.mult, ALU.add))
                dve.wait_ge(placed, 1)
                lk(dve.tensor_tensor(tmp[:, :, :], ps_p[:, 0:T * E].rearrange("p (t e) -> p t e", e=E),
                                     room[:, None, :].to_broadcast([P, T, E]), ALU.is_lt))
                lk(dve.tensor_tensor(tie[:, :, :], tie[:, :, :], tmp[:, :, :], ALU.mult))
                lk(dve.tensor_tensor(over[:, :, :], over[:, :, :], tie[:, :, :], ALU.add))
                lk(dve.tensor_copy(keptb[:, :, :], over[:, :, :]))
                dve.sem_inc(kept_ready, 1)
                dve.wait_ge(placed, 2)
                lk(dve.tensor_tensor(slot[:, :, :], ps_p[:, 0:T * E].rearrange("p (t e) -> p t e", e=E),
                                     first[:, None, :].to_broadcast([P, T, E]), ALU.add))
                for c in range(TOP):
                    lk(dve.tensor_scalar(choice[:, :, :], rank[:, :, :], float(c), None, ALU.is_equal))
                    lk(dve.tensor_tensor(choice[:, :, :], choice[:, :, :], over[:, :, :], ALU.mult))
                    lk(dve.tensor_reduce(kept[:, :], choice[:, :, :], AX, ALU.add))
                    lk(dve.tensor_tensor(tmp[:, :, :], choice[:, :, :], prob[:, :, :], ALU.mult))
                    lk(dve.tensor_reduce(gate[:, c, :], tmp[:, :, :], AX, ALU.add))
                    lk(dve.tensor_tensor(tmp[:, :, :], choice[:, :, :], slot[:, :, :], ALU.mult))
                    lk(dve.tensor_reduce(dest[:, :], tmp[:, :, :], AX, ALU.add))
                    dve.tensor_copy(place[:, c, :], dest[:, :])
                    lk(dve.tensor_scalar(kept[:, :], kept[:, :], -float(FAR), float(FAR), ALU.mult, ALU.add))
                    lk(dve.tensor_tensor(dest[:, :], dest[:, :], kept[:, :], ALU.add))
                    lk(dve.tensor_copy(index[:, c, :], dest[:, :]))
                    dve.sem_inc(index_ready, 1)

            @block.tensor
            def _(pe):
                pe.wait_ge(setup, 5 + E)
                for n in range(len(BITS) + 1):
                    pe.wait_ge(hit_ready, n + 1)
                    pe.matmul(ps_c[:, 0:T * E], onesb[:, :], flat(hit), start=True, stop=True).then_inc(counted, 1)
                for n in range(2):
                    pe.wait_ge(kept_ready, n + 1)
                    pe.matmul(ps_p[:, 0:T * E], before[:, :], flat(keptb), start=True, stop=False)
                    for t in range(T - 1):
                        mm = pe.matmul(ps_p[:, (t + 1) * E:T * E].rearrange("p (t e) -> p t e", e=E), onesb[:, :],
                                       keptb[:, t:t + 1, :].to_broadcast([P, T - 1 - t, E]),
                                       start=False, stop=(t == T - 2))
                    mm.then_inc(placed, 1)


FK = FFN // P
ST = CAP // P
HC = CAP // 2


def stage_experts(nc, sem, keep, w1, w2, xe_dram, ye_dram):
    ident = keep["ident"]
    with Stage(nc, "e") as st:
        w1r, w2r = st.sb("w1r", [P, KD, FFN]), st.sb("w2r", [P, FK, D])
        w1s = [st.sb(f"w1{n}", [P, KD, FFN], F32R) for n in ("h", "l")]
        w2s = [st.sb(f"w2{n}", [P, FK, D], F32R) for n in ("h", "l")]
        xe = st.sb("xe", [P, ST, D])
        xT = [st.sb(f"xT{n}", [P, KD, CAP], F32R) for n in ("h", "l")]
        hT = [st.sb(f"hT{n}", [P, FK, CAP], F32R) for n in ("h", "l")]
        ye = [st.sb(f"ye{i}", [P, D]) for i in range(2)]
        ps_h = [st.ps(f"h{i}", [P, BANK]) for i in range(4)]
        ps_t = [st.ps(f"t{i}", [P, BANK]) for i in range(2)]
        ps_y = [st.ps(f"y{i}", [P, BANK]) for i in range(2)]
        w1_in, w2_in, xe_in = sem("e_w1_in"), sem("e_w2_in"), sem("e_xe_in")
        w1_high, w1_ready, w2_high, w2_ready = (sem("e_" + n) for n in ("w1h", "w1r", "w2h", "w2r"))
        w1_used, w2_used = sem("e_w1_used"), sem("e_w2_used")
        x_full, x_high, x_ready = sem("e_xf"), sem("e_xh"), sem("e_xr")
        h_full, h_high, h_ready = sem("e_hf"), sem("e_hh"), sem("e_hr")
        y_full, y_ready = sem("e_yf"), sem("e_yr")
        y_sent = [sem(f"e_ys{i}") for i in range(2)]
        PARTS = ((0, 0), (0, 1), (1, 0))
        HN = 2 * FK
        w1c = lambda a, n: a[:, n, :]
        w2c = lambda a, n: a[:, 2 * n:2 * n + 2, :]
        with nc.Block() as block:

            @block.sync
            def _(sp):
                def load(e, first=False):
                    if not first:
                        sp.wait_ge(w1_ready, e * 4)
                    sp.dma_start(w1r[:, :, :], w1[ds(e, 1), :, :].rearrange("e (k p) f -> p (e k) f", p=P)).then_inc(w1_in, 16)
                    if not first:
                        sp.wait_ge(x_full, e * ST)
                    sp.dma_start(xe[:, :, :], xe_dram[ds(e * CAP, CAP), :].rearrange("(s p) d -> p s d", p=P)).then_inc(xe_in, 16)
                    if not first:
                        sp.wait_ge(w2_ready, e * 4)
                    sp.dma_start(w2r[:, :, :], w2[ds(e, 1), :, :].rearrange("e (f p) d -> p (e f) d", p=P)).then_inc(w2_in, 16)

                load(0, first=True)
                with sp.Fori(1, EXPERTS) as e:
                    load(e)

            @block.gpsimd
            def _(pool):
                with pool.Fori(0, EXPERTS) as e:
                    for s in range(ST):
                        pool.wait_ge(y_ready, e * ST + s + 1)
                        pool.dma_start(ye_dram[ds(e * CAP + s * P, P), :], ye[s % 2][:, :]).then_inc(y_sent[s % 2], 16)
                        pool.wait_ge(y_sent[s % 2], e * (16 * (3 if s % 2 == 0 else 2)) + 16 * (s // 2 + 1))

            def split_plan(eng, which, e, n, high):
                raw, parts, cut, arrived, used, hs, rs = (
                    (w1r, w1s, w1c, w1_in, w1_used, w1_high, w1_ready) if which == 1 else
                    (w2r, w2s, w2c, w2_in, w2_used, w2_high, w2_ready))
                if high:
                    if n == 0:
                        eng.wait_ge(arrived, e * 16 + 16)
                        eng.wait_ge(used, e + 1)
                    eng.activation(cut(parts[0], n), cut(raw, n), ACT.Copy).then_inc(hs, 1)
                else:
                    eng.wait_ge(hs, e * 4 + n + 1)
                    eng.tensor_tensor(cut(parts[1], n), cut(raw, n), cut(parts[0], n).bitcast(F32),
                                      ALU.subtract).then_inc(rs, 1)

            @block.scalar
            def _(act):
                def inputs(e):
                    for n in range(4):
                        split_plan(act, 1, e, n, True)
                    for s in range(ST):
                        act.wait_ge(x_full, e * ST + s + 1)
                        act.activation(xT[0][:, :, s * P:(s + 1) * P],
                                       ps_t[s % 2][:, :].rearrange("p (k q) -> p k q", q=P), ACT.Copy).then_inc(x_high, 1)

                def hidden(e):
                    for n in range(HN):
                        if n % 4 == 0:
                            split_plan(act, 2, e, n // 4, True)
                        act.wait_ge(h_full, e * HN + n + 1)
                        f, half = n // 2, n % 2
                        act.activation(hT[0][:, f, half * HC:(half + 1) * HC], ps_h[n % 4][:, 0:HC], ACT.Relu).then_inc(h_high, 1)

                inputs(0)
                with act.Fori(0, EXPERTS - 1) as e:
                    hidden(e)
                    inputs(e + 1)
                hidden(EXPERTS - 1)

            @block.vector
            def _(dve):
                def inputs(e):
                    for n in range(4):
                        split_plan(dve, 1, e, n, False)
                    for s in range(ST):
                        dve.wait_ge(x_high, e * ST + s + 1)
                        cut = xT[0][:, :, s * P:(s + 1) * P]
                        dve.tensor_tensor(xT[1][:, :, s * P:(s + 1) * P],
                                          ps_t[s % 2][:, :].rearrange("p (k q) -> p k q", q=P), cut.bitcast(F32),
                                          ALU.subtract).then_inc(x_ready, 1)

                def hidden(e):
                    for n in range(HN):
                        if n % 4 == 0:
                            split_plan(dve, 2, e, n // 4, False)
                        dve.wait_ge(h_high, e * HN + n + 1)
                        f, half = n // 2, n % 2
                        cut = slice(half * HC, (half + 1) * HC)
                        dve.scalar_tensor_tensor(hT[1][:, f, cut], ps_h[n % 4][:, 0:HC], 0.0,
                                                 hT[0][:, f, cut].bitcast(F32), ALU.max, ALU.subtract).then_inc(h_ready, 1)

                def outputs(e, first=False):
                    for s in range(ST):
                        dve.wait_ge(y_full, e * ST + s + 1)
                        if s >= 2:
                            dve.wait_ge(y_sent[s % 2], e * (16 * (3 if s % 2 == 0 else 2)) + 16 * (s // 2))
                        elif not first:
                            dve.wait_ge(y_sent[s % 2], e * (16 * (3 if s % 2 == 0 else 2)))
                        dve.tensor_copy(ye[s % 2][:, :], ps_y[s % 2][:, :]).then_inc(y_ready, 1)

                inputs(0)
                hidden(0)
                inputs(1)
                outputs(0, first=True)
                with dve.Fori(1, EXPERTS - 1) as e:
                    hidden(e)
                    inputs(e + 1)
                    outputs(e)
                hidden(EXPERTS - 1)
                outputs(EXPERTS - 1)

            @block.tensor
            def _(pe):
                pe.sem_inc(w1_used, 1)
                pe.sem_inc(w2_used, 1)

                def turn(e, first=False):
                    pe.wait_ge(xe_in, e * 16 + 16)
                    for s in range(ST):
                        if s >= 2:
                            pe.wait_ge(x_ready, e * ST + s - 1)
                        elif not first:
                            pe.wait_ge(x_ready, e * ST)
                        for k in range(KD):
                            mm = pe.transpose(ps_t[s % 2][:, k * P:(k + 1) * P], xe[:, s, k * P:(k + 1) * P], ident[:, :])
                        mm.then_inc(x_full, 1)

                def hidden(e, first=False):
                    for n in range(HN):
                        f, half = n // 2, n % 2
                        if n == 0:
                            pe.wait_ge(x_ready, e * ST + ST)
                            pe.wait_ge(w1_ready, e * 4 + 4)
                        if n >= 4:
                            pe.wait_ge(h_ready, e * HN + n - 3)
                        elif not first:
                            pe.wait_ge(h_ready, e * HN)
                        m = 0
                        for k in range(KD):
                            for wp, xp in PARTS:
                                mm = pe.matmul(ps_h[n % 4][:, 0:HC], w1s[wp][:, k, f * P:(f + 1) * P],
                                               xT[xp][:, k, half * HC:(half + 1) * HC],
                                               start=(m == 0), stop=(m == 3 * KD - 1))
                                m += 1
                        mm.then_inc(h_full, 1)
                    pe.wait_ge(h_full, e * HN + HN)
                    pe.sem_inc(w1_used, 1)

                def outputs(e, first=False):
                    pe.wait_ge(h_ready, e * HN + HN)
                    pe.wait_ge(w2_ready, e * 4 + 4)
                    for s in range(ST):
                        if s >= 2:
                            pe.wait_ge(y_ready, e * ST + s - 1)
                        elif not first:
                            pe.wait_ge(y_ready, e * ST)
                        m = 0
                        for f in range(FK):
                            for wp, hp in PARTS:
                                mm = pe.matmul(ps_y[s % 2][:, :], hT[hp][:, f, s * P:(s + 1) * P], w2s[wp][:, f, :],
                                               start=(m == 0), stop=(m == 3 * FK - 1))
                                m += 1
                        mm.then_inc(y_full, 1)
                    pe.wait_ge(y_full, e * ST + ST)
                    pe.sem_inc(w2_used, 1)

                turn(0, first=True)
                hidden(0, first=True)
                turn(1)
                outputs(0, first=True)
                with pe.Fori(1, EXPERTS - 1) as e:
                    hidden(e)
                    turn(e + 1)
                    outputs(e)
                hidden(EXPERTS - 1)
                outputs(EXPERTS - 1)


def stage_combine(nc, sem, keep, res_dram, ye_dram, out):
    gate, place = keep["gate"], keep["place"]
    R = 4
    with Stage(nc, "c") as st:
        base = st.sb("base", [P, T, D])
        part = [[st.sb(f"part{i}{c}", [P, D]) for c in range(TOP)] for i in range(R)]
        base_in = [sem(f"c_base_in{i}") for i in range(4)]
        got = [sem(f"c_got{i}") for i in range(R)]
        link, used, done, sent = (sem("c_" + n) for n in ("link", "used", "done", "sent"))
        rv = res_dram.rearrange("(t p) d -> p t d", p=P)
        ov = out.rearrange("(t p) d -> p t d", p=P)
        with nc.Block() as block:

            @block.sync
            def _(sp):
                for c in range(4):
                    sp.dma_start(base[:, 4 * c:4 * c + 4, :], rv[:, 4 * c:4 * c + 4, :]).then_inc(base_in[c], 16)
                for t in range(0, T, 2):
                    sp.wait_ge(done, t + 2)
                    sp.dma_start(ov[:, t:t + 2, :], base[:, t:t + 2, :]).then_inc(sent, 16)
                sp.wait_ge(sent, 16 * T // 2)

            @block.gpsimd
            def _(pool):
                for t in range(T):
                    if t >= R:
                        pool.wait_ge(used, t - R + 1)
                    for c in range(TOP):
                        pool.indirect_dma_start(out=part[t % R][c][:, :], out_offset=None, in_=ye_dram,
                                                in_offset=bass.IndirectOffsetOnAxis(ap=place[:, c, t:t + 1], axis=0),
                                                bounds_check=EXPERTS * CAP - 1, oob_is_err=False).then_inc(got[t % R], 16)

            @block.vector
            def _(dve):
                lk = Link(dve, link)
                for t in range(T):
                    if t % 4 == 0:
                        dve.wait_ge(base_in[t // 4], 16)
                    dve.wait_ge(got[t % R], 32 * (t // R + 1))
                    for c in range(TOP):
                        lk(dve.scalar_tensor_tensor(base[:, t, :], part[t % R][c][:, :], gate[:, c, t:t + 1],
                                                    base[:, t, :], ALU.mult, ALU.add))
                    dve.sem_inc(used, 1)
                    dve.sem_inc(done, 1)


def constants():
    theta = (10000.0 ** (-2.0 * (np.arange(DH // 2) / DH))).astype(np.float32)
    angle = np.arange(N, dtype=np.float32)[:, None] * theta[None, :]
    cos = np.repeat(np.cos(angle).astype(np.float32).T, 2, axis=0)
    sin = np.repeat(np.sin(angle).astype(np.float32).T, 2, axis=0)
    sin[0::2] *= np.float32(-1.0)
    return {"cos": np.tile(cos, (4, 1)), "sin": np.tile(sin, (4, 1))}


def program(nc, ins, outs, scratch, upto=99):
    sems = {}
    ctx = ExitStack()
    with ctx:
        def sem(name):
            if name not in sems:
                sems[name] = nc.alloc_semaphore(name=name)
            return sems[name]

        def recycle():
            nc.clear_and_free_semaphores(list(sems.values()))
            sems.clear()
            nc.all_engine_barrier()

        keep = {"consts_ready": sem("consts_ready")}
        with Stage(nc, "all") as whole:
            keep["ident"], keep["ident_b"] = whole.sb("ident", [P, P]), whole.sb("ident_b", [P, P], BF16)
            keep["prob"] = whole.sb("prob", [P, T, EXPERTS])
            keep["gate"], keep["place"] = whole.sb("gate", [P, TOP, T]), whole.sb("place", [P, TOP, T], U32)
            with Stage(nc, "k") as k:
                keep["part"] = k.sb("part", [P, T, H, W1])
                rows = keep["part"][:, :, :, :].rearrange("p t h c -> p (t h c)")[:, 0:T * D]
                keep["V"] = keep["Z"] = rows.rearrange("p (t d) -> p t d", t=T)
                with Stage(nc, "gat") as gat:
                    keep["seq"] = gat.sb("seq", [P, T, D])
                    keep["adjT"] = gat.sb("adjT", [P, T, N], BF16)
                    for n in ("s1", "s2", "ns2", "A", "B", "C", "D"):
                        keep[n] = gat.sb(n, [P, T, H])
                    stage_sequence(nc, sem, keep, ins["x"], ins["adj"], ins["L0_gnn_W_seq"], ins["L0_gnn_a1"],
                                   ins["L0_gnn_a2"])
                    stage_factors(nc, sem, keep, scratch["s1"])
                    stage_adjacency_product(nc, sem, keep)
                    stage_masks(nc, sem, keep, scratch["s1"])
                recycle()
                keep["X1"] = k.sb("X1", [P, T, D])
                keep["mv"], keep["rstd"] = k.sb("mv", [P, T, 2]), k.sb("rstd", [P, T])
                with Stage(nc, "proj") as pr:
                    keep["xgT"] = pr.sb("xgT", [P, KD, N])
                    stage_gnn_output(nc, sem, keep, ins["x"], ins["L0_gnn_W_out"], ins["L0_gnn_b_out"],
                                     ins["L0_ffn_g1"], scratch["xe"])
                    stage_qkv(nc, sem, keep, ins["L0_ffn_w_qkv"], ins["cos"], ins["sin"], scratch["parts"])
                stage_attention(nc, sem, keep, scratch["parts"], scratch["o"])
                recycle()
                stage_router(nc, sem, keep, ins["L0_ffn_w_o"], ins["L0_ffn_g2"], ins["L0_ffn_w_router"],
                             scratch["o"], scratch["rec"], scratch["res"])
                stage_slots(nc, sem, keep, scratch["xe"])
            stage_experts(nc, sem, keep, ins["L0_ffn_w1"], ins["L0_ffn_w2"], scratch["xe"], scratch["ye"])
            stage_combine(nc, sem, keep, scratch["res"], scratch["ye"], outs[0])


SCRATCH = {"s1": ((2 * P, P), F32), "parts": ((4, D, N), F32), "o": ((H * (DH + 1), N), F32), "rec": ((H, N), F32), "res": ((N, D), F32),
           "xe": ((EXPERTS * CAP, D), F32), "ye": ((EXPERTS * CAP, D), F32)}
NAMES = ["x", "adj", "L0_gnn_W_seq", "L0_gnn_a1", "L0_gnn_a2", "L0_gnn_W_out", "L0_gnn_b_out", "L0_ffn_g1",
         "L0_ffn_w_qkv", "L0_ffn_w_o", "L0_ffn_g2", "L0_ffn_w_router", "L0_ffn_w1", "L0_ffn_w2"]


def kernel(**inputs):
    from concourse import bacc
    from concourse.bass_utils import run_bass_kernel_spmd

    nc = bacc.Bacc("TRN2", target_bir_lowering=False, num_devices=1)
    arrays = {n: np.ascontiguousarray(inputs[n]) for n in NAMES}
    arrays.update(constants())
    ins = {n: nc.dram_tensor(f"in_{n}", a.shape, mybir.dt.from_np(a.dtype), kind="ExternalInput").ap()
           for n, a in arrays.items()}
    out = nc.dram_tensor("out", (N, D), F32, kind="ExternalOutput").ap()
    scratch = {n: nc.dram_tensor(f"scratch_{n}", shape, dt).ap() for n, (shape, dt) in SCRATCH.items()}
    program(nc, ins, [out], scratch)
    result = run_bass_kernel_spmd(nc, [{f"in_{n}": a for n, a in arrays.items()}], core_ids=[0])
    return result.results[0]["out"]
```
